# Optimizing a Trainium2 kernel written in Bass

```python
import numpy as np
import jax
import jax.numpy as jnp

def _softmax(x, axis=-1):
    return jax.nn.softmax(x, axis=axis)

def _gelu(x):
    return jax.nn.gelu(x, approximate=True)

def _silu(x):
    return jax.nn.silu(x)

def _sigmoid(x):
    return jax.nn.sigmoid(x)

def _layernorm(x, axis=-1, eps=1e-05):
    m = jnp.mean(x, axis=axis, keepdims=True)
    v = jnp.var(x, axis=axis, keepdims=True)
    return (x - m) / jnp.sqrt(v + eps)

def _scatter_add(tgt, idx, src, axis=0):
    return tgt.at[idx].add(src)

def _segment_sum(src, seg, n):
    return jax.ops.segment_sum(src, seg, n)
kernel_name = 'mk_pixart_seq_d4_seqx_r8_5ee1e1'

def setup_inputs(seed: int=0):
    np.random.seed(seed)
    _w = jnp.asarray

    def _rec_inputs():
        import jax
        import jax.numpy as jnp
        _rk = jax.random.key(seed)
        x = -0.0002928 + 1 * jax.random.normal(jax.random.fold_in(_rk, 1), (16, 128, 128), jnp.float32)
        _lenS = 128 - jax.random.randint(jax.random.fold_in(_rk, 7), (16,), 0, max(1, 128 // 4) + 1, jnp.int32)
        _lenS2 = 77 - jax.random.randint(jax.random.fold_in(_rk, 8), (16,), 0, max(1, 77 // 4) + 1, jnp.int32)
        cond_1024 = 0.0061147 + 1.02565 * jax.random.normal(jax.random.fold_in(_rk, 11), (16, 128), jnp.float32)
        _ctx_1024P = jax.random.normal(jax.random.fold_in(_rk, 12), (16, 16, 128), jnp.float32)
        _ctx_1024c = jax.random.dirichlet(jax.random.fold_in(_rk, 512), 0.3 * jnp.ones((16,), jnp.float32), (16, 77))
        _ctx_1024t = jnp.einsum('bsk,bkd->bsd', _ctx_1024c, _ctx_1024P)
        _ctx_1024t = _ctx_1024t * jax.lax.rsqrt(jnp.mean(jnp.square(_ctx_1024t)) + 1e-12) * 0.953939
        ctx_1024 = -0.00265004 + 0.998804 * (_ctx_1024t + 0.3 * jax.random.normal(jax.random.fold_in(_rk, 612), (16, 77, 128), jnp.float32))
        _validS = jnp.arange(128)[None, :] < _lenS[:, None]
        _validS2 = jnp.arange(77)[None, :] < _lenS2[:, None]
        _causal = jnp.tril(jnp.ones((128, 128), dtype=bool))
        mask_BxS2_bf1 = jnp.ones((16, 77), dtype=bool)
        mask_SxS_bk0 = jnp.logical_not(jnp.broadcast_to(_validS[0:1, :], (128, 128)))
        return (x, cond_1024, ctx_1024, mask_BxS2_bf1, mask_SxS_bk0)
    x, cond_1024, ctx_1024, mask_BxS2_bf1, mask_SxS_bk0 = _rec_inputs()

    def _L0_xcond_setup():
        import jax, jax.numpy as jnp
        import numpy as np
        LN_EPS = 1e-06

        def _ln(x):
            mu = jnp.mean(x, axis=-1, keepdims=True)
            var = jnp.var(x, axis=-1, keepdims=True)
            return (x - mu) * jax.lax.rsqrt(var + LN_EPS)
        key = jax.random.key(seed)
        H, NH = (128, 16)
        B, N, S = (4, 128, 77)
        MLP = int(H * 4.0)
        ks = jax.random.split(key, 20)
        s = 1.0 / np.sqrt(H)
        return {'x': jax.random.normal(ks[0], (B, N, H), jnp.float32), 'c': jax.random.normal(ks[1], (B, H), jnp.float32), 'context': jax.random.normal(ks[2], (B, S, H), jnp.float32), 'W_mod': jax.random.normal(ks[3], (H, 6 * H), jnp.float32) * s, 'b_mod': jnp.zeros((6 * H,), jnp.float32), 'W_qkv': jax.random.normal(ks[4], (H, 3 * H), jnp.float32) * s, 'b_qkv': jnp.zeros((3 * H,), jnp.float32), 'W_proj': jax.random.normal(ks[5], (H, H), jnp.float32) * s, 'b_proj': jnp.zeros((H,), jnp.float32), 'W_qc': jax.random.normal(ks[6], (H, H), jnp.float32) * s, 'b_qc': jnp.zeros((H,), jnp.float32), 'W_kvc': jax.random.normal(ks[7], (H, 2 * H), jnp.float32) * s, 'b_kvc': jnp.zeros((2 * H,), jnp.float32), 'W_cproj': jax.random.normal(ks[8], (H, H), jnp.float32) * s, 'b_cproj': jnp.zeros((H,), jnp.float32), 'W_mlp1': jax.random.normal(ks[9], (H, MLP), jnp.float32) * s, 'b_mlp1': jnp.zeros((MLP,), jnp.float32), 'W_mlp2': jax.random.normal(ks[10], (MLP, H), jnp.float32) * (1.0 / np.sqrt(MLP)), 'b_mlp2': jnp.zeros((H,), jnp.float32)}
    _L0_xcond_all = _L0_xcond_setup()
    _L0_xcond_in = {k: v for k, v in _L0_xcond_all.items() if k in ('W_mod', 'b_mod', 'W_qkv', 'b_qkv', 'W_proj', 'b_proj', 'W_qc', 'b_qc', 'W_kvc', 'b_kvc', 'W_cproj', 'b_cproj', 'W_mlp1', 'b_mlp1', 'W_mlp2', 'b_mlp2')}
    del _L0_xcond_all

    def _L1_xcond_setup():
        import jax, jax.numpy as jnp
        import numpy as np
        D = 128
        H = 16
        HD = D // H
        MLP = 4 * D
        EPS = 1e-06
        SCALE = HD ** (-0.5)

        def _p(key, shape, s=0.02):
            return jax.random.normal(key, shape, dtype=jnp.float32) * s

        def _ln(x):
            mu = jnp.mean(x, axis=-1, keepdims=True)
            var = jnp.var(x, axis=-1, keepdims=True)
            return (x - mu) * jax.lax.rsqrt(var + EPS)

        def _heads(t):
            B, L, _ = t.shape
            return t.reshape(B, L, H, HD).transpose(0, 2, 1, 3)

        def _attend(q, k, v):
            attn = jnp.einsum('bhnd,bhsd->bhns', q, k) * SCALE
            attn = jax.nn.softmax(attn, axis=-1)
            o = jnp.einsum('bhns,bhsd->bhnd', attn, v)
            B, _, N, _ = q.shape
            return o.transpose(0, 2, 1, 3).reshape(B, N, D)
        key = jax.random.key(seed)
        ks = jax.random.split(key, 24)
        B, N, S = (4, 128, 77)
        return {'x': jax.random.normal(ks[0], (B, N, D), dtype=jnp.float32), 't_emb': jax.random.normal(ks[1], (B, D), dtype=jnp.float32), 'context': jax.random.normal(ks[2], (B, S, D), dtype=jnp.float32), 'adaln_w': _p(ks[3], (D, 6 * D)), 'adaln_b': _p(ks[4], (6 * D,)), 'qkv_w': _p(ks[5], (D, 3 * D)), 'qkv_b': _p(ks[6], (3 * D,)), 'sa_proj_w': _p(ks[7], (D, D)), 'sa_proj_b': _p(ks[8], (D,)), 'q_w': _p(ks[9], (D, D)), 'q_b': _p(ks[10], (D,)), 'kv_w': _p(ks[11], (D, 2 * D)), 'kv_b': _p(ks[12], (2 * D,)), 'ca_proj_w': _p(ks[13], (D, D)), 'ca_proj_b': _p(ks[14], (D,)), 'fc1_w': _p(ks[15], (D, MLP)), 'fc1_b': _p(ks[16], (MLP,)), 'fc2_w': _p(ks[17], (MLP, D)), 'fc2_b': _p(ks[18], (D,))}
    _L1_xcond_all = _L1_xcond_setup()
    _L1_xcond_in = {k: v for k, v in _L1_xcond_all.items() if k in ('adaln_w', 'adaln_b', 'qkv_w', 'qkv_b', 'sa_proj_w', 'sa_proj_b', 'q_w', 'q_b', 'kv_w', 'kv_b', 'ca_proj_w', 'ca_proj_b', 'fc1_w', 'fc1_b', 'fc2_w', 'fc2_b')}
    del _L1_xcond_all

    def _L2_xcond_setup():
        import jax, jax.numpy as jnp
        import numpy as np
        import math
        D_MODEL = 128
        N_HEADS = 16
        HEAD_DIM = D_MODEL // N_HEADS
        D_FF = 512
        EPS = 1e-05
        ROPE_BASE = 10000.0

        def _rope(t):
            L, Dh = (t.shape[1], t.shape[-1])
            half = Dh // 2
            inv_freq = 1.0 / ROPE_BASE ** (jnp.arange(half, dtype=t.dtype) / half)
            ang = jnp.arange(L, dtype=t.dtype)[:, None] * inv_freq[None, :]
            cos = jnp.cos(ang)[None, :, None, :]
            sin = jnp.sin(ang)[None, :, None, :]
            t1, t2 = (t[..., :half], t[..., half:])
            return jnp.concatenate([t1 * cos - t2 * sin, t2 * cos + t1 * sin], axis=-1)

        def _adaln(x, emb, w, b):
            e = emb[:, 0, :]
            gb = e @ w.T + b
            gamma, beta = jnp.split(gb, 2, axis=-1)
            mu = x.mean(-1, keepdims=True)
            var = x.var(-1, keepdims=True)
            xn = (x - mu) * jax.lax.rsqrt(var + EPS)
            return xn * (1.0 + gamma[:, None, :]) + beta[:, None, :]

        def _attn(q, k, v):
            scale = 1.0 / math.sqrt(HEAD_DIM)
            scores = jnp.einsum('bqhd,bkhd->bhqk', q, k) * scale
            w = jax.nn.softmax(scores, axis=-1)
            out = jnp.einsum('bhqk,bkhd->bqhd', w, v)
            B, Lq = (out.shape[0], out.shape[1])
            return out.reshape(B, Lq, D_MODEL)
        key = jax.random.key(seed)
        ks = jax.random.split(key, 24)
        s = 0.02
        inp = {'x': jax.random.normal(ks[0], (2, 256, D_MODEL), jnp.float32), 'noise_emb': jax.random.normal(ks[1], (2, 1, D_MODEL), jnp.float32), 'context': jax.random.normal(ks[2], (2, 128, D_MODEL), jnp.float32), 'ln1_w': jax.random.normal(ks[3], (2 * D_MODEL, D_MODEL), jnp.float32) * s, 'ln1_b': jax.random.normal(ks[4], (2 * D_MODEL,), jnp.float32) * s, 'ln2_w': jax.random.normal(ks[5], (2 * D_MODEL, D_MODEL), jnp.float32) * s, 'ln2_b': jax.random.normal(ks[6], (2 * D_MODEL,), jnp.float32) * s, 'ln3_w': jax.random.normal(ks[7], (2 * D_MODEL, D_MODEL), jnp.float32) * s, 'ln3_b': jax.random.normal(ks[8], (2 * D_MODEL,), jnp.float32) * s, 'qkv_w': jax.random.normal(ks[9], (3 * D_MODEL, D_MODEL), jnp.float32) * s, 'sa_out_w': jax.random.normal(ks[10], (D_MODEL, D_MODEL), jnp.float32) * s, 'q_w': jax.random.normal(ks[11], (D_MODEL, D_MODEL), jnp.float32) * s, 'k_w': jax.random.normal(ks[12], (D_MODEL, D_MODEL), jnp.float32) * s, 'v_w': jax.random.normal(ks[13], (D_MODEL, D_MODEL), jnp.float32) * s, 'ca_out_w': jax.random.normal(ks[14], (D_MODEL, D_MODEL), jnp.float32) * s, 'ffn_w1': jax.random.normal(ks[15], (D_FF, D_MODEL), jnp.float32) * s, 'ffn_b1': jax.random.normal(ks[16], (D_FF,), jnp.float32) * s, 'ffn_w2': jax.random.normal(ks[17], (D_MODEL, D_FF), jnp.float32) * s, 'ffn_b2': jax.random.normal(ks[18], (D_MODEL,), jnp.float32) * s}
        return inp
    _L2_xcond_all = _L2_xcond_setup()
    _L2_xcond_in = {k: v for k, v in _L2_xcond_all.items() if k in ('ln1_w', 'ln1_b', 'ln2_w', 'ln2_b', 'ln3_w', 'ln3_b', 'qkv_w', 'sa_out_w', 'q_w', 'k_w', 'v_w', 'ca_out_w', 'ffn_w1', 'ffn_b1', 'ffn_w2', 'ffn_b2')}
    del _L2_xcond_all

    def _L3_xcond_setup():
        import jax, jax.numpy as jnp
        import numpy as np
        B, N, D, H, LC = (2, 128, 128, 16, 77)
        HD = D // H
        BLOCK = 16
        ROPE_BASE = 10000.0
        EPS = 1e-05

        def _block_diff_mask(n, block_size):
            idx = np.arange(2 * n)
            q = idx[:, None]
            kv = idx[None, :]
            fq = q >= n
            fkv = kv >= n
            bq = np.where(fq, (q - n) // block_size, q // block_size)
            bkv = np.where(fkv, (kv - n) // block_size, kv // block_size)
            block_diagonal = (bq == bkv) & (fq == fkv)
            offset_block_causal = (bq > bkv) & fkv & ~fq
            block_causal = (bq >= bkv) & fq & fkv
            return jnp.asarray(block_diagonal | offset_block_causal | block_causal)

        def _rope_tables(n):
            inv_freq = 1.0 / ROPE_BASE ** (np.arange(0, HD, 2, dtype=np.float32) / HD)
            freqs = np.outer(np.arange(n, dtype=np.float32), inv_freq)
            emb = np.concatenate([freqs, freqs], axis=-1)
            cos = jnp.asarray(np.cos(emb), jnp.float32)[None, :, None, :]
            sin = jnp.asarray(np.sin(emb), jnp.float32)[None, :, None, :]
            return (cos, sin)

        def _ln(x, w):
            xf = x.astype(jnp.float32)
            mu = jnp.mean(xf, axis=-1, keepdims=True)
            var = jnp.mean(jnp.square(xf - mu), axis=-1, keepdims=True)
            y = (xf - mu) * jax.lax.rsqrt(var + EPS)
            return y * w[None, None, :]

        def _apply_rope(t, cos, sin):
            t1, t2 = jnp.split(t, 2, axis=-1)
            rot = jnp.concatenate([-t2, t1], axis=-1)
            return t * cos + rot * sin

        def _attn(q, k, v, mask):
            scale = 1.0 / np.sqrt(HD)
            s = jnp.einsum('bqhd,bkhd->bhqk', q, k) * scale
            s = jnp.where(mask, s, jnp.finfo(s.dtype).min)
            a = jax.nn.softmax(s, axis=-1)
            return jnp.einsum('bhqk,bkhd->bqhd', a, v)
        key = jax.random.key(seed)
        ks = jax.random.split(key, 16)
        w = lambda k, shp: jax.random.normal(k, shp, jnp.float32) * 0.02
        inp = {'x': jax.random.normal(ks[0], (B, 2 * N, D), jnp.float32), 'cond_global': jax.random.normal(ks[1], (B, D), jnp.float32), 'cond_tokens': jax.random.normal(ks[2], (B, LC, D), jnp.float32), 'adaLN_W': w(ks[3], (D, 9 * D)), 'adaLN_b': w(ks[4], (9 * D,)), 'norm1_w': jnp.ones((D,), jnp.float32), 'qkv_W': w(ks[5], (D, 3 * D)), 'attn_out_W': w(ks[6], (D, D)), 'normc_w': jnp.ones((D,), jnp.float32), 'cq_W': w(ks[7], (D, D)), 'ck_W': w(ks[8], (D, D)), 'cv_W': w(ks[9], (D, D)), 'co_W': w(ks[10], (D, D)), 'norm2_w': jnp.ones((D,), jnp.float32), 'mlp_W1': w(ks[11], (D, 4 * D)), 'mlp_b1': w(ks[12], (4 * D,)), 'mlp_W2': w(ks[13], (4 * D, D)), 'mlp_b2': w(ks[14], (D,)), 'cond_kv_mask': jnp.ones((B, LC), bool), 'attn_mask': _block_diff_mask(N, BLOCK)}
        return inp
    _L3_xcond_all = _L3_xcond_setup()
    _L3_xcond_in = {k: v for k, v in _L3_xcond_all.items() if k in ('adaLN_W', 'adaLN_b', 'norm1_w', 'qkv_W', 'attn_out_W', 'normc_w', 'cq_W', 'ck_W', 'cv_W', 'co_W', 'norm2_w', 'mlp_W1', 'mlp_b1', 'mlp_W2', 'mlp_b2')}
    del _L3_xcond_all
    return {'x': x, 'cond_1024': cond_1024, 'ctx_1024': ctx_1024, 'mask_BxS2_bf1': mask_BxS2_bf1, 'mask_SxS_bk0': mask_SxS_bk0, 'L0_xcond_W_mod': _L0_xcond_in['W_mod'], 'L0_xcond_b_mod': _L0_xcond_in['b_mod'], 'L0_xcond_W_qkv': _L0_xcond_in['W_qkv'], 'L0_xcond_b_qkv': _L0_xcond_in['b_qkv'], 'L0_xcond_W_proj': _L0_xcond_in['W_proj'], 'L0_xcond_b_proj': _L0_xcond_in['b_proj'], 'L0_xcond_W_qc': _L0_xcond_in['W_qc'], 'L0_xcond_b_qc': _L0_xcond_in['b_qc'], 'L0_xcond_W_kvc': _L0_xcond_in['W_kvc'], 'L0_xcond_b_kvc': _L0_xcond_in['b_kvc'], 'L0_xcond_W_cproj': _L0_xcond_in['W_cproj'], 'L0_xcond_b_cproj': _L0_xcond_in['b_cproj'], 'L0_xcond_W_mlp1': _L0_xcond_in['W_mlp1'], 'L0_xcond_b_mlp1': _L0_xcond_in['b_mlp1'], 'L0_xcond_W_mlp2': _L0_xcond_in['W_mlp2'], 'L0_xcond_b_mlp2': _L0_xcond_in['b_mlp2'], 'L1_xcond_adaln_w': _L1_xcond_in['adaln_w'], 'L1_xcond_adaln_b': _L1_xcond_in['adaln_b'], 'L1_xcond_qkv_w': _L1_xcond_in['qkv_w'], 'L1_xcond_qkv_b': _L1_xcond_in['qkv_b'], 'L1_xcond_sa_proj_w': _L1_xcond_in['sa_proj_w'], 'L1_xcond_sa_proj_b': _L1_xcond_in['sa_proj_b'], 'L1_xcond_q_w': _L1_xcond_in['q_w'], 'L1_xcond_q_b': _L1_xcond_in['q_b'], 'L1_xcond_kv_w': _L1_xcond_in['kv_w'], 'L1_xcond_kv_b': _L1_xcond_in['kv_b'], 'L1_xcond_ca_proj_w': _L1_xcond_in['ca_proj_w'], 'L1_xcond_ca_proj_b': _L1_xcond_in['ca_proj_b'], 'L1_xcond_fc1_w': _L1_xcond_in['fc1_w'], 'L1_xcond_fc1_b': _L1_xcond_in['fc1_b'], 'L1_xcond_fc2_w': _L1_xcond_in['fc2_w'], 'L1_xcond_fc2_b': _L1_xcond_in['fc2_b'], 'L2_xcond_ln1_w': _L2_xcond_in['ln1_w'], 'L2_xcond_ln1_b': _L2_xcond_in['ln1_b'], 'L2_xcond_ln2_w': _L2_xcond_in['ln2_w'], 'L2_xcond_ln2_b': _L2_xcond_in['ln2_b'], 'L2_xcond_ln3_w': _L2_xcond_in['ln3_w'], 'L2_xcond_ln3_b': _L2_xcond_in['ln3_b'], 'L2_xcond_qkv_w': _L2_xcond_in['qkv_w'], 'L2_xcond_sa_out_w': _L2_xcond_in['sa_out_w'], 'L2_xcond_q_w': _L2_xcond_in['q_w'], 'L2_xcond_k_w': _L2_xcond_in['k_w'], 'L2_xcond_v_w': _L2_xcond_in['v_w'], 'L2_xcond_ca_out_w': _L2_xcond_in['ca_out_w'], 'L2_xcond_ffn_w1': _L2_xcond_in['ffn_w1'], 'L2_xcond_ffn_b1': _L2_xcond_in['ffn_b1'], 'L2_xcond_ffn_w2': _L2_xcond_in['ffn_w2'], 'L2_xcond_ffn_b2': _L2_xcond_in['ffn_b2'], 'L3_xcond_adaLN_W': _L3_xcond_in['adaLN_W'], 'L3_xcond_adaLN_b': _L3_xcond_in['adaLN_b'], 'L3_xcond_norm1_w': _L3_xcond_in['norm1_w'], 'L3_xcond_qkv_W': _L3_xcond_in['qkv_W'], 'L3_xcond_attn_out_W': _L3_xcond_in['attn_out_W'], 'L3_xcond_normc_w': _L3_xcond_in['normc_w'], 'L3_xcond_cq_W': _L3_xcond_in['cq_W'], 'L3_xcond_ck_W': _L3_xcond_in['ck_W'], 'L3_xcond_cv_W': _L3_xcond_in['cv_W'], 'L3_xcond_co_W': _L3_xcond_in['co_W'], 'L3_xcond_norm2_w': _L3_xcond_in['norm2_w'], 'L3_xcond_mlp_W1': _L3_xcond_in['mlp_W1'], 'L3_xcond_mlp_b1': _L3_xcond_in['mlp_b1'], 'L3_xcond_mlp_W2': _L3_xcond_in['mlp_W2'], 'L3_xcond_mlp_b2': _L3_xcond_in['mlp_b2']}

def reference(x, cond_1024, ctx_1024, mask_BxS2_bf1, mask_SxS_bk0, L0_xcond_W_mod, L0_xcond_b_mod, L0_xcond_W_qkv, L0_xcond_b_qkv, L0_xcond_W_proj, L0_xcond_b_proj, L0_xcond_W_qc, L0_xcond_b_qc, L0_xcond_W_kvc, L0_xcond_b_kvc, L0_xcond_W_cproj, L0_xcond_b_cproj, L0_xcond_W_mlp1, L0_xcond_b_mlp1, L0_xcond_W_mlp2, L0_xcond_b_mlp2, L1_xcond_adaln_w, L1_xcond_adaln_b, L1_xcond_qkv_w, L1_xcond_qkv_b, L1_xcond_sa_proj_w, L1_xcond_sa_proj_b, L1_xcond_q_w, L1_xcond_q_b, L1_xcond_kv_w, L1_xcond_kv_b, L1_xcond_ca_proj_w, L1_xcond_ca_proj_b, L1_xcond_fc1_w, L1_xcond_fc1_b, L1_xcond_fc2_w, L1_xcond_fc2_b, L2_xcond_ln1_w, L2_xcond_ln1_b, L2_xcond_ln2_w, L2_xcond_ln2_b, L2_xcond_ln3_w, L2_xcond_ln3_b, L2_xcond_qkv_w, L2_xcond_sa_out_w, L2_xcond_q_w, L2_xcond_k_w, L2_xcond_v_w, L2_xcond_ca_out_w, L2_xcond_ffn_w1, L2_xcond_ffn_b1, L2_xcond_ffn_w2, L2_xcond_ffn_b2, L3_xcond_adaLN_W, L3_xcond_adaLN_b, L3_xcond_norm1_w, L3_xcond_qkv_W, L3_xcond_attn_out_W, L3_xcond_normc_w, L3_xcond_cq_W, L3_xcond_ck_W, L3_xcond_cv_W, L3_xcond_co_W, L3_xcond_norm2_w, L3_xcond_mlp_W1, L3_xcond_mlp_b1, L3_xcond_mlp_W2, L3_xcond_mlp_b2):
    import jax
    import jax.numpy as jnp

    def _L0_xcond_ref(x, c, context, W_mod, b_mod, W_qkv, b_qkv, W_proj, b_proj, W_qc, b_qc, W_kvc, b_kvc, W_cproj, b_cproj, W_mlp1, b_mlp1, W_mlp2, b_mlp2):
        import jax, jax.numpy as jnp
        import numpy as np
        LN_EPS = 1e-06

        def _ln(x):
            mu = jnp.mean(x, axis=-1, keepdims=True)
            var = jnp.var(x, axis=-1, keepdims=True)
            return (x - mu) * jax.lax.rsqrt(var + LN_EPS)
        B, N, H = x.shape
        NH = 16
        hd = H // NH
        scale = hd ** (-0.5)
        c_proj = jax.nn.silu(c) @ W_mod + b_mod
        shift_a, scale_a, gate_a, shift_m, scale_m, gate_m = jnp.split(c_proj, 6, axis=-1)

        def modulate(t, shift, sc):
            return t * (1 + sc[:, None]) + shift[:, None]
        x_norm = modulate(_ln(x), shift_a, scale_a)
        qkv = x_norm @ W_qkv + b_qkv
        q, k, v = jnp.split(qkv, 3, axis=-1)
        q = q.reshape(B, N, NH, hd).transpose(0, 2, 1, 3)
        k = k.reshape(B, N, NH, hd).transpose(0, 2, 1, 3)
        v = v.reshape(B, N, NH, hd).transpose(0, 2, 1, 3)
        attn_w = jax.nn.softmax(jnp.einsum('bhqd,bhkd->bhqk', q, k) * scale, axis=-1)
        attn_out = jnp.einsum('bhqk,bhkd->bhqd', attn_w, v)
        attn_out = attn_out.transpose(0, 2, 1, 3).reshape(B, N, H)
        attn_out = attn_out @ W_proj + b_proj
        x = x + gate_a[:, None] * attn_out
        S = context.shape[1]
        q_c = _ln(x) @ W_qc + b_qc
        kv_c = _ln(context) @ W_kvc + b_kvc
        k_c, v_c = jnp.split(kv_c, 2, axis=-1)
        q_c = q_c.reshape(B, N, NH, hd).transpose(0, 2, 1, 3)
        k_c = k_c.reshape(B, S, NH, hd).transpose(0, 2, 1, 3)
        v_c = v_c.reshape(B, S, NH, hd).transpose(0, 2, 1, 3)
        c_attn_w = jax.nn.softmax(jnp.einsum('bhqd,bhsd->bhqs', q_c, k_c) * scale, axis=-1)
        c_attn_out = jnp.einsum('bhqs,bhsd->bhqd', c_attn_w, v_c)
        c_attn_out = c_attn_out.transpose(0, 2, 1, 3).reshape(B, N, H)
        c_attn_out = c_attn_out @ W_cproj + b_cproj
        x = x + c_attn_out
        x_norm2 = modulate(_ln(x), shift_m, scale_m)
        h = jax.nn.gelu(x_norm2 @ W_mlp1 + b_mlp1)
        h = h @ W_mlp2 + b_mlp2
        x = x + gate_m[:, None] * h
        return x

    def _L1_xcond_ref(x, t_emb, context, adaln_w, adaln_b, qkv_w, qkv_b, sa_proj_w, sa_proj_b, q_w, q_b, kv_w, kv_b, ca_proj_w, ca_proj_b, fc1_w, fc1_b, fc2_w, fc2_b):
        import jax, jax.numpy as jnp
        import numpy as np
        D = 128
        H = 16
        HD = D // H
        MLP = 4 * D
        EPS = 1e-06
        SCALE = HD ** (-0.5)

        def _p(key, shape, s=0.02):
            return jax.random.normal(key, shape, dtype=jnp.float32) * s

        def _ln(x):
            mu = jnp.mean(x, axis=-1, keepdims=True)
            var = jnp.var(x, axis=-1, keepdims=True)
            return (x - mu) * jax.lax.rsqrt(var + EPS)

        def _heads(t):
            B, L, _ = t.shape
            return t.reshape(B, L, H, HD).transpose(0, 2, 1, 3)

        def _attend(q, k, v):
            attn = jnp.einsum('bhnd,bhsd->bhns', q, k) * SCALE
            attn = jax.nn.softmax(attn, axis=-1)
            o = jnp.einsum('bhns,bhsd->bhnd', attn, v)
            B, _, N, _ = q.shape
            return o.transpose(0, 2, 1, 3).reshape(B, N, D)
        B, N, _ = x.shape
        S = context.shape[1]
        mod = jax.nn.silu(t_emb) @ adaln_w + adaln_b
        sh_sa, sc_sa, g_sa, sh_ff, sc_ff, g_ff = jnp.split(mod[:, None, :], 6, axis=-1)
        xm = _ln(x) * (1.0 + sc_sa) + sh_sa
        qkv = (xm @ qkv_w + qkv_b).reshape(B, N, 3, H, HD)
        q = qkv[:, :, 0].transpose(0, 2, 1, 3)
        k = qkv[:, :, 1].transpose(0, 2, 1, 3)
        v = qkv[:, :, 2].transpose(0, 2, 1, 3)
        x_sa = _attend(q, k, v) @ sa_proj_w + sa_proj_b
        x = x + g_sa * x_sa
        xn = _ln(x)
        q = _heads(xn @ q_w + q_b)
        kv = (context @ kv_w + kv_b).reshape(B, S, 2, H, HD)
        k = kv[:, :, 0].transpose(0, 2, 1, 3)
        v = kv[:, :, 1].transpose(0, 2, 1, 3)
        x_ca = _attend(q, k, v) @ ca_proj_w + ca_proj_b
        x = x + x_ca
        xm = _ln(x) * (1.0 + sc_ff) + sh_ff
        h = jax.nn.gelu(xm @ fc1_w + fc1_b, approximate=True)
        x_ff = h @ fc2_w + fc2_b
        x = x + g_ff * x_ff
        return x

    def _L2_xcond_ref(x, noise_emb, context, ln1_w, ln1_b, ln2_w, ln2_b, ln3_w, ln3_b, qkv_w, sa_out_w, q_w, k_w, v_w, ca_out_w, ffn_w1, ffn_b1, ffn_w2, ffn_b2):
        import jax, jax.numpy as jnp
        import numpy as np
        import math
        D_MODEL = 128
        N_HEADS = 16
        HEAD_DIM = D_MODEL // N_HEADS
        D_FF = 512
        EPS = 1e-05
        ROPE_BASE = 10000.0

        def _rope(t):
            L, Dh = (t.shape[1], t.shape[-1])
            half = Dh // 2
            inv_freq = 1.0 / ROPE_BASE ** (jnp.arange(half, dtype=t.dtype) / half)
            ang = jnp.arange(L, dtype=t.dtype)[:, None] * inv_freq[None, :]
            cos = jnp.cos(ang)[None, :, None, :]
            sin = jnp.sin(ang)[None, :, None, :]
            t1, t2 = (t[..., :half], t[..., half:])
            return jnp.concatenate([t1 * cos - t2 * sin, t2 * cos + t1 * sin], axis=-1)

        def _adaln(x, emb, w, b):
            e = emb[:, 0, :]
            gb = e @ w.T + b
            gamma, beta = jnp.split(gb, 2, axis=-1)
            mu = x.mean(-1, keepdims=True)
            var = x.var(-1, keepdims=True)
            xn = (x - mu) * jax.lax.rsqrt(var + EPS)
            return xn * (1.0 + gamma[:, None, :]) + beta[:, None, :]

        def _attn(q, k, v):
            scale = 1.0 / math.sqrt(HEAD_DIM)
            scores = jnp.einsum('bqhd,bkhd->bhqk', q, k) * scale
            w = jax.nn.softmax(scores, axis=-1)
            out = jnp.einsum('bhqk,bkhd->bqhd', w, v)
            B, Lq = (out.shape[0], out.shape[1])
            return out.reshape(B, Lq, D_MODEL)
        B, L, D = x.shape
        L_ctx = context.shape[1]
        res = x
        xn = _adaln(x, noise_emb, ln1_w, ln1_b)
        qkv = xn @ qkv_w.T
        q, k, v = jnp.split(qkv, 3, axis=-1)
        q = _rope(q.reshape(B, L, N_HEADS, HEAD_DIM))
        k = _rope(k.reshape(B, L, N_HEADS, HEAD_DIM))
        v = v.reshape(B, L, N_HEADS, HEAD_DIM)
        sa = _attn(q, k, v) @ sa_out_w.T
        x = res + sa
        res = x
        xn = _adaln(x, noise_emb, ln2_w, ln2_b)
        q = _rope((xn @ q_w.T).reshape(B, L, N_HEADS, HEAD_DIM))
        k = _rope((context @ k_w.T).reshape(B, L_ctx, N_HEADS, HEAD_DIM))
        v = (context @ v_w.T).reshape(B, L_ctx, N_HEADS, HEAD_DIM)
        ca = _attn(q, k, v) @ ca_out_w.T
        x = res + ca
        res = x
        xn = _adaln(x, noise_emb, ln3_w, ln3_b)
        h = jax.nn.gelu(xn @ ffn_w1.T + ffn_b1, approximate=False)
        x = res + (h @ ffn_w2.T + ffn_b2)
        return x

    def _L3_xcond_ref(x, cond_global, cond_tokens, adaLN_W, adaLN_b, norm1_w, qkv_W, attn_out_W, normc_w, cq_W, ck_W, cv_W, co_W, norm2_w, mlp_W1, mlp_b1, mlp_W2, mlp_b2, cond_kv_mask, attn_mask):
        import jax, jax.numpy as jnp
        import numpy as np
        B, N, D, H, LC = (2, 128, 128, 16, 77)
        HD = D // H
        BLOCK = 16
        ROPE_BASE = 10000.0
        EPS = 1e-05

        def _block_diff_mask(n, block_size):
            idx = np.arange(2 * n)
            q = idx[:, None]
            kv = idx[None, :]
            fq = q >= n
            fkv = kv >= n
            bq = np.where(fq, (q - n) // block_size, q // block_size)
            bkv = np.where(fkv, (kv - n) // block_size, kv // block_size)
            block_diagonal = (bq == bkv) & (fq == fkv)
            offset_block_causal = (bq > bkv) & fkv & ~fq
            block_causal = (bq >= bkv) & fq & fkv
            return jnp.asarray(block_diagonal | offset_block_causal | block_causal)

        def _rope_tables(n):
            inv_freq = 1.0 / ROPE_BASE ** (np.arange(0, HD, 2, dtype=np.float32) / HD)
            freqs = np.outer(np.arange(n, dtype=np.float32), inv_freq)
            emb = np.concatenate([freqs, freqs], axis=-1)
            cos = jnp.asarray(np.cos(emb), jnp.float32)[None, :, None, :]
            sin = jnp.asarray(np.sin(emb), jnp.float32)[None, :, None, :]
            return (cos, sin)

        def _ln(x, w):
            xf = x.astype(jnp.float32)
            mu = jnp.mean(xf, axis=-1, keepdims=True)
            var = jnp.mean(jnp.square(xf - mu), axis=-1, keepdims=True)
            y = (xf - mu) * jax.lax.rsqrt(var + EPS)
            return y * w[None, None, :]

        def _apply_rope(t, cos, sin):
            t1, t2 = jnp.split(t, 2, axis=-1)
            rot = jnp.concatenate([-t2, t1], axis=-1)
            return t * cos + rot * sin

        def _attn(q, k, v, mask):
            scale = 1.0 / np.sqrt(HD)
            s = jnp.einsum('bqhd,bkhd->bhqk', q, k) * scale
            s = jnp.where(mask, s, jnp.finfo(s.dtype).min)
            a = jax.nn.softmax(s, axis=-1)
            return jnp.einsum('bhqk,bkhd->bqhd', a, v)
        b, s, d = x.shape
        n = s // 2
        mod = (cond_global @ adaLN_W + adaLN_b)[:, None, :]
        sh_msa, sc_msa, g_msa, sh_x, sc_x, g_x, sh_mlp, sc_mlp, g_mlp = jnp.split(mod, 9, axis=-1)
        x_norm = _ln(x, norm1_w) * (1 + sc_msa) + sh_msa
        cos, sin = _rope_tables(n)

        def qkv(h):
            t = (h @ qkv_W).reshape(b, n, 3, H, HD)
            q, k, v = (t[:, :, 0], t[:, :, 1], t[:, :, 2])
            return (_apply_rope(q, cos, sin), _apply_rope(k, cos, sin), v)
        q1, k1, v1 = qkv(x_norm[:, :n])
        q2, k2, v2 = qkv(x_norm[:, n:])
        q = jnp.concatenate([q1, q2], axis=1)
        k = jnp.concatenate([k1, k2], axis=1)
        v = jnp.concatenate([v1, v2], axis=1)
        self_out = _attn(q, k, v, attn_mask[None, None]).reshape(b, s, d) @ attn_out_W
        x = x + g_msa * self_out
        xc = _ln(x, normc_w) * (1 + sc_x) + sh_x
        qc = (xc @ cq_W).reshape(b, s, H, HD)
        kc = (cond_tokens @ ck_W).reshape(b, LC, H, HD)
        vc = (cond_tokens @ cv_W).reshape(b, LC, H, HD)
        cross = _attn(qc, kc, vc, cond_kv_mask[:, None, None, :]).reshape(b, s, d) @ co_W
        x = x + g_x * cross
        xm = _ln(x, norm2_w) * (1 + sc_mlp) + sh_mlp
        h = jax.nn.gelu(xm @ mlp_W1 + mlp_b1, approximate=True)
        mlp_out = h @ mlp_W2 + mlp_b2
        return x + g_mlp * mlp_out
    x = _L0_xcond_ref(x, cond_1024, ctx_1024, L0_xcond_W_mod, L0_xcond_b_mod, L0_xcond_W_qkv, L0_xcond_b_qkv, L0_xcond_W_proj, L0_xcond_b_proj, L0_xcond_W_qc, L0_xcond_b_qc, L0_xcond_W_kvc, L0_xcond_b_kvc, L0_xcond_W_cproj, L0_xcond_b_cproj, L0_xcond_W_mlp1, L0_xcond_b_mlp1, L0_xcond_W_mlp2, L0_xcond_b_mlp2)
    x = _L1_xcond_ref(x, cond_1024, ctx_1024, L1_xcond_adaln_w, L1_xcond_adaln_b, L1_xcond_qkv_w, L1_xcond_qkv_b, L1_xcond_sa_proj_w, L1_xcond_sa_proj_b, L1_xcond_q_w, L1_xcond_q_b, L1_xcond_kv_w, L1_xcond_kv_b, L1_xcond_ca_proj_w, L1_xcond_ca_proj_b, L1_xcond_fc1_w, L1_xcond_fc1_b, L1_xcond_fc2_w, L1_xcond_fc2_b)
    x = _L2_xcond_ref(x, cond_1024[:, None, :], ctx_1024, L2_xcond_ln1_w, L2_xcond_ln1_b, L2_xcond_ln2_w, L2_xcond_ln2_b, L2_xcond_ln3_w, L2_xcond_ln3_b, L2_xcond_qkv_w, L2_xcond_sa_out_w, L2_xcond_q_w, L2_xcond_k_w, L2_xcond_v_w, L2_xcond_ca_out_w, L2_xcond_ffn_w1, L2_xcond_ffn_b1, L2_xcond_ffn_w2, L2_xcond_ffn_b2)
    x = _L3_xcond_ref(x, cond_1024, ctx_1024, L3_xcond_adaLN_W, L3_xcond_adaLN_b, L3_xcond_norm1_w, L3_xcond_qkv_W, L3_xcond_attn_out_W, L3_xcond_normc_w, L3_xcond_cq_W, L3_xcond_ck_W, L3_xcond_cv_W, L3_xcond_co_W, L3_xcond_norm2_w, L3_xcond_mlp_W1, L3_xcond_mlp_b1, L3_xcond_mlp_W2, L3_xcond_mlp_b2, mask_BxS2_bf1, mask_SxS_bk0)
    return x

_drawn_inputs = setup_inputs


def setup_inputs(seed=0):
    import zlib

    import numpy as np

    out = dict(_drawn_inputs(seed))
    spreads = {'L0_xcond_b_mod': (0.0, 0.1),
     'L0_xcond_b_qkv': (0.0, 0.1),
     'L0_xcond_b_proj': (0.0, 0.1),
     'L0_xcond_b_qc': (0.0, 0.492),
     'L0_xcond_b_kvc': (0.0, 0.1),
     'L0_xcond_b_cproj': (0.0, 0.1),
     'L0_xcond_b_mlp1': (0.0, 0.1),
     'L0_xcond_b_mlp2': (0.0, 0.1),
     'L3_xcond_norm1_w': (1.0, 0.6),
     'L3_xcond_normc_w': (1.0, 0.6),
     'L3_xcond_norm2_w': (1.0, 0.6)}
    factors = {'L1_xcond_adaln_w': 8.0,
     'L1_xcond_adaln_b': 8.0,
     'L1_xcond_qkv_w': 8.0,
     'L1_xcond_qkv_b': 8.0,
     'L1_xcond_sa_proj_w': 8.0,
     'L1_xcond_sa_proj_b': 8.0,
     'L1_xcond_q_w': 24.139,
     'L1_xcond_q_b': 64.0,
     'L1_xcond_kv_w': 2.742,
     'L1_xcond_kv_b': 30.078,
     'L1_xcond_ca_proj_w': 2.785,
     'L1_xcond_ca_proj_b': 16.945,
     'L1_xcond_fc1_w': 8.0,
     'L1_xcond_fc1_b': 8.0,
     'L1_xcond_fc2_w': 8.0,
     'L1_xcond_fc2_b': 27.385,
     'L2_xcond_ln1_w': 35.02,
     'L2_xcond_ln1_b': 64.0,
     'L2_xcond_ln2_w': 34.254,
     'L2_xcond_ln2_b': 200.0,
     'L2_xcond_ln3_w': 32.029,
     'L2_xcond_ln3_b': 64.0,
     'L2_xcond_q_w': 31.734,
     'L2_xcond_k_w': 31.646,
     'L2_xcond_v_w': 9.369,
     'L2_xcond_ca_out_w': 9.859,
     'L2_xcond_ffn_b1': 64.0,
     'L2_xcond_ffn_b2': 100.21,
     'L3_xcond_adaLN_W': 4.162,
     'L3_xcond_adaLN_b': 8.0,
     'L3_xcond_qkv_W': 7.248,
     'L3_xcond_attn_out_W': 6.69,
     'L3_xcond_cq_W': 8.0,
     'L3_xcond_ck_W': 8.0,
     'L3_xcond_cv_W': 8.0,
     'L3_xcond_co_W': 8.0,
     'L3_xcond_mlp_W1': 5.779,
     'L3_xcond_mlp_b1': 22.24,
     'L3_xcond_mlp_W2': 5.648,
     'L3_xcond_mlp_b2': 42.628,
     'L2_xcond_qkv_w': 5.626,
     'L2_xcond_sa_out_w': 5.813,
     'L2_xcond_ffn_w1': 6.095,
     'L2_xcond_ffn_w2': 5.378}
    for name, (base, spread) in spreads.items():
        noise = np.random.default_rng([zlib.crc32(name.encode()), seed]).standard_normal(out[name].shape)
        drawn = base * np.exp(spread * noise) if base else spread * noise
        out[name] = jnp.asarray(drawn.astype(out[name].dtype))
    for name, factor in factors.items():
        out[name] = (out[name] * factor).astype(out[name].dtype)
    return out
```

```python
from contextlib import ExitStack

import numpy as np

import concourse.bass as bass
from concourse import mybir

ALU = mybir.AluOpType
ACT = mybir.ActivationFunctionType
AX = mybir.AxisListType
F32 = mybir.dt.float32
BF16 = mybir.dt.bfloat16
U8 = mybir.dt.uint8

B, N, D = 16, 128, 128
H, HD = 16, 8
C = 77
FF = 512
GB = 4
GROUPS = B // GB
TOK = GB * N
HG = 4
NHG = H // HG
VW = HD + 1
SCALE = float(HD) ** -0.5
BIG = 3.3895313892515355e38

SELF, CROSS, MLP = range(3)


def phase(kind, layer, **more):
    p = dict(kind=kind, layer=layer, mod=None, gate=None, bias=None, qbias=None, kbias=None, vbias=None,
             rope=None, krope=False, mask=False, eps=1e-6, gelu=None)
    p.update(more)
    return p


PHASES = [
    phase(SELF, 0, mod=0, gate=0, bias=0, qbias=0, kbias=1, vbias=8),
    phase(CROSS, 0, bias=1, qbias=2, kbias=3, vbias=9),
    phase(MLP, 0, mod=1, gate=1, bias=2, gelu="tanh"),
    phase(SELF, 1, mod=2, gate=2, bias=3, qbias=4, kbias=5, vbias=10),
    phase(CROSS, 1, bias=4, qbias=6, kbias=7, vbias=11),
    phase(MLP, 1, mod=3, gate=3, bias=5, gelu="tanh"),
    phase(SELF, 2, mod=4, rope=0, eps=1e-5),
    phase(CROSS, 2, mod=5, rope=0, eps=1e-5),
    phase(MLP, 2, mod=6, bias=6, eps=1e-5, gelu="erf"),
    phase(SELF, 3, mod=7, gate=4, rope=1, mask=True, eps=1e-5),
    phase(CROSS, 3, mod=8, gate=5, mask=True, eps=1e-5),
    phase(MLP, 3, mod=9, gate=6, bias=7, eps=1e-5, gelu="tanh"),
]
NMOD, NGATE, NBIAS, NLAYER = 10, 7, 12, 4
a = m = r = 0
for p_ in PHASES:
    p_["n0"] = 4 * PHASES.index(p_)
    p_["u0"], p_["m0"], p_["r0"] = a, m, r
    a += GROUPS * (p_["kind"] != MLP)
    m += GROUPS * (p_["kind"] == MLP)
    r += GROUPS * (p_["rope"] is not None)

WQ, WK, WV, WO, CQ, CK, CV, CO, W1, W2, WEND = np.cumsum([0] + [D] * 8 + [FF, FF]).tolist()
ROT = {(SELF, 2): (0, D), (CROSS, 2): (2 * D, 3 * D), (SELF, 3): (4 * D, 5 * D)}
NROT = 6


def build(nc, x, cond_t, ctx_tok, ctx_t, w, wrot, modw, modb, gatew, gateb, normw, colb, rowb, mlpb,
          smask, cmask, cmask_t, ident, identb, jmask8, jmask4, sel, ropec, ropes, out):
    with ExitStack() as ctx:
        def sb(name, shape, dt=F32):
            return ctx.enter_context(nc.sbuf_tensor(name, shape, dt))

        def sem(name):
            return ctx.enter_context(nc.semaphore(name))

        X = sb("X", [N, B, D])
        W = sb("W", [D, NLAYER, WEND])
        WR = sb("WR", [D, NROT * D])
        GATE = sb("GATE", [N, NGATE, B, D])
        SCL = sb("SCL", [D, NMOD, B])
        SHF = sb("SHF", [D, NMOD, B])
        CTXT = sb("CTXT", [D, B * C])
        CTXN = sb("CTXN", [D, B * C])
        COLB = sb("COLB", [D, 8])
        ROWB = sb("ROWB", [N, NBIAS, D])
        MLPB = sb("MLPB", [D, NLAYER, FF // D])
        ID = sb("ID", [N, N])
        IDB = sb("IDB", [N, N], BF16)
        J8 = sb("J8", [D, HG])
        J4 = sb("J4", [D, HG])
        SEL = sb("SEL", [D, GB * NHG, N], BF16)
        RC = sb("RC", [D, 2, N])
        RS = sb("RS", [D, 2, N])
        SM = sb("SM", [N, N], BF16)
        CM = sb("CM", [N, B, C], BF16)
        CMT = sb("CMT", [C, B])
        ONE = sb("ONE", [N, N], BF16)
        NHALF = sb("NHALF", [N, GB])
        EPS = sb("EPS", [N, 2, GB])
        CMG = sb("CMG", [N, GB, C], BF16)
        CMTG = sb("CMTG", [C, GB])
        XN = sb("XN", [N, GB, D])
        ST = sb("STAT", [N, GB, 6])
        HOLD = sb("HOLD", [N, 1])
        MV = sb("MV", [N, GB, 2])
        VE = sb("VE", [N, GB])
        RSTD = sb("RSTD", [N, GB])
        XNT = sb("XNT", [D, TOK])
        CG = sb("CG", [D, GB * C])
        QT = sb("QT", [D, TOK])
        KT = sb("KT", [D, TOK])
        T1 = sb("T1", [D, TOK])
        T2 = sb("T2", [D, TOK])
        QBD = sb("QBD", [D, HG, TOK])
        VX = sb("VX", [N, GB, H, VW])
        MX = sb("MX", [N, GB * H])
        MHL = sb("MHL", [N, 2, GB * H], BF16)
        MBD = sb("MBD", [N, HG, N], BF16)
        PR = sb("PR", [N, 2, H * N])
        HT = PR[:, 0, :].rearrange("p (c t) -> p c t", c=FF // D)
        RDEN = sb("RDEN", [N, H])
        OQ = sb("OQ", [N, 2, D])
        OT = sb("OT", [D, GB, N])
        YT = sb("YT", [N, GB, D])
        CRAW = PR[:, 0, :].rearrange("p (b d) -> p b d", b=B)
        CS = sb("CS", [D, 2, B])
        CT = sb("CT", [D, 3, B])
        MODW = PR[:, 1, :]
        MODB = sb("MODB", [D, 2 * NMOD])
        GATEW = sb("GATEW", [D, NGATE * D])
        G = sb("G", [B, 2, NGATE * D])
        NORMW = sb("NORMW", [D, 3])
        MU8 = sb("MU8", [N, N + B], U8)
        CM8 = sb("CM8", [1, B * C], U8)
        gate_dram = nc.dram_tensor("gate_rows", (B, NGATE * D), F32, kind="Internal").ap()

        SC = ctx.enter_context(nc.psum_tensor("SC", [N, 4, 512], F32))
        PX = ctx.enter_context(nc.psum_tensor("PX", [N, 512], F32))
        PO = ctx.enter_context(nc.psum_tensor("PO", [N, 512], F32))
        PY = ctx.enter_context(nc.psum_tensor("PY", [N, 512], F32))
        PV = ctx.enter_context(nc.psum_tensor("PV", [N, 512], F32))
        PXB = PX[:, 0:64].bitcast(BF16)

        names = ("cond_in mods_in gatew_in small_in ctx_in ctxt_in const_in wrot_in gate_out gate_in out_done "
                 "silu_exp silu_step cond_ready mod_psum mod_step mods_ready g_psum g_ready mask_ready const_set "
                 "ln_stats ln_moments var_eps rstd_ready xn_ready xnt_psum xnt_ready cg_ready cm_ready "
                 "q_psum k_psum v_psum rope_parts qt_ready kt_ready v_ready qbd_ready "
                 "s_psum mx_ready neg_hi neg_ready m_psum mbd_ready st_psum p_ready o_psum rden_ready "
                 "oq_ready ot_psum ot_ready y_psum yt_ready gated x_ready h_psum h_ready wq_scaled "
                 "cstats cmoments cvar crstd cn_ready ct_psum ct_ready").split()
        S = {k: sem("s_" + k) for k in names}
        x_in = [sem(f"s_x_in{i}") for i in range(GROUPS)]
        w_in = [sem(f"s_w_in{i}") for i in range(NLAYER)]
        block = ctx.enter_context(nc.Block())

        def wl(layer, at, width=D):
            return W[:, layer, at:at + width]

        def loop(eng):
            return eng.Fori(0, GROUPS)

        def weights(p):
            own = p["kind"] == SELF
            return (WQ, WK, WV, WO) if own else (CQ, CK, CV, CO)

        def keys(p):
            return N if p["kind"] == SELF else C

        @block.sync
        def _(sp):
            sp.dma_start(CS[:, 1, :], cond_t).then_inc(S["cond_in"], 16)
            sp.dma_start(CRAW[0:C, :, :], ctx_tok.rearrange("b c d -> c b d")).then_inc(S["ctx_in"], 16)
            for i in range(GROUPS):
                sp.dma_start(X[:, GB * i:GB * i + GB, :],
                             x[GB * i:GB * i + GB].rearrange("b t d -> t b d")).then_inc(x_in[i], 16)
            sp.dma_start(CTXT[:, :], ctx_t).then_inc(S["ctxt_in"], 16)
            for layer in range(NLAYER):
                sp.dma_start(W[:, layer, :], w[layer]).then_inc(w_in[layer], 16)
            sp.dma_start(WR[:, :], wrot).then_inc(S["wrot_in"], 16)
            sp.wait_ge(S["g_ready"], 2)
            sp.dma_start(gate_dram, G[:, 1, :]).then_inc(S["gate_out"], 16)
            sp.wait_ge(S["gate_out"], 16)
            for g in range(NGATE):
                sp.dma_start(GATE[:, g, :, :],
                             gate_dram[:, g * D:g * D + D].partition_broadcast(N)).then_inc(S["gate_in"], 16)
            last = PHASES[-1]
            with loop(sp) as i:
                sp.wait_ge(S["x_ready"], last["n0"] + 1 + i)
                sp.dma_start(out[bass.ds(GB * i, GB)].rearrange("b t d -> t b d"),
                             X[:, bass.ds(GB * i, GB), :]).then_inc(S["out_done"], 16)
            sp.wait_ge(S["out_done"], 16 * GROUPS)

        @block.scalar
        def _(act):
            for dst, src in ((ID[:, :], ident), (IDB[:, :], identb), (J8[:, :], jmask8), (J4[:, :], jmask4),
                             (SEL[:, :, :], sel), (RC[:, :, :], ropec), (RS[:, :, :], ropes)):
                act.dma_start(dst, src).then_inc(S["const_in"], 16)
            act.dma_start(MODB[:, :], modb).then_inc(S["small_in"], 16)
            act.dma_start(NORMW[:, :], normw).then_inc(S["small_in"], 16)
            act.dma_start(COLB[:, :], colb).then_inc(S["small_in"], 16)
            act.dma_start(MLPB[:, :, :], mlpb).then_inc(S["small_in"], 16)
            act.dma_start(ROWB[:, :, :], rowb.partition_broadcast(N)).then_inc(S["small_in"], 16)
            act.dma_start(MU8[:, 0:N], smask).then_inc(S["small_in"], 16)
            act.dma_start(MU8[0:C, N:N + B], cmask_t).then_inc(S["small_in"], 16)
            act.dma_start(CM8[:, :], cmask).then_inc(S["small_in"], 16)
            act.dma_start(GATEW[:, :], gatew).then_inc(S["gatew_in"], 16)
            act.dma_start(G[:, 0, :], gateb.partition_broadcast(B)).then_inc(S["gatew_in"], 16)
            act.wait_ge(S["cond_in"], 16)
            act.activation(CT[:, 0, :], CS[:, 1, :], ACT.Exp, scale=-1.0).then_inc(S["silu_exp"], 1)
            for part in range(2):
                if part:
                    act.wait_ge(S["mod_psum"], 1)
                act.dma_start(MODW[:, 0:NMOD * D], modw[:, part * NMOD * D:(part + 1) * NMOD * D])\
                   .then_inc(S["mods_in"], 16)

            act.wait_ge(S["ct_psum"], 1)
            with loop(act) as i:
                act.wait_ge(S["ct_psum"], i + 1)
                act.activation(CTXN[:, bass.ds(GB * C * i, GB * C)], PX[:, 0:GB * C], ACT.Copy).then_inc(S["ct_ready"], 1)

            def normed(p, i):
                act.wait_ge(S["xnt_psum"], p["n0"] + 1 + i)
                if p["mod"] is None:
                    act.activation(XNT[:, :], PX[:, :], ACT.Copy).then_inc(S["xnt_ready"], GB)
                    return
                for b in range(GB):
                    s = bass.ds(GB * i + b, 1)
                    act.activation(XNT[:, b * N:b * N + N], PX[:, b * N:b * N + N], ACT.Identity,
                                   bias=SHF[:, p["mod"], s], scale=SCL[:, p["mod"], s]).then_inc(S["xnt_ready"], 1)

            def attention(p, i):
                u, T = p["u0"] + i, keys(p)
                normed(p, i)
                if p["rope"] is None:
                    act.wait_ge(S["q_psum"], u + 1)
                    if p["qbias"] is None:
                        act.activation(QT[:, :], SC[:, 0, :], ACT.Copy).then_inc(S["qt_ready"], 1)
                    else:
                        act.activation(QT[:, :], SC[:, 0, :], ACT.Identity,
                                       bias=COLB[:, p["qbias"]:p["qbias"] + 1]).then_inc(S["qt_ready"], 1)
                act.wait_ge(S["qt_ready"], u + 1)
                for j in range(2, HG):
                    act.activation(QBD[:, j, :], QT[:, :], ACT.Identity, scale=J8[:, j:j + 1])\
                       .then_inc(S["qbd_ready"], 1)
                if p["mask"] and p["kind"] == CROSS:
                    act.wait_ge(S["cm_ready"], 2 * (i + 1))

                def transposed(b):
                    act.wait_ge(S["ot_psum"], 4 * u + b + 1)
                    act.activation(OT[:, b, :], PX[:, 0:N], ACT.Copy).then_inc(S["ot_ready"], 1)

                for b in range(GB):
                    if b >= 2:
                        act.wait_ge(S["o_psum"], 4 * u + b - 1)
                    for pr in range(2):
                        act.wait_ge(S["st_psum"], 8 * u + 2 * b + pr + 1)
                        more = {}
                        if p["mask"] and p["kind"] == CROSS:
                            more = dict(bias=CMTG[:, b:b + 1])
                        act.activation(PR[0:T, b % 2, pr * 1024:pr * 1024 + 1024], SC[0:T, 2 * pr:2 * pr + 2, :],
                                       ACT.Exp, **more).then_inc(S["p_ready"], 1)
                    if b >= 2:
                        transposed(b - 2)
                transposed(GB - 2)
                transposed(GB - 1)

            def mlp(p, i):
                m = p["m0"] + i
                normed(p, i)
                f = ACT.Gelu if p["gelu"] == "erf" else ACT.Gelu_apprx_tanh
                for c in range(FF // D):
                    act.wait_ge(S["h_psum"], 4 * m + c + 1)
                    act.activation(HT[:, c, :], SC[:, c, :], f,
                                   bias=MLPB[:, p["layer"], c:c + 1]).then_inc(S["h_ready"], 1)

            act.wait_ge(S["mods_ready"], 1)
            act.wait_ge(S["const_in"], 16 * 7)
            act.wait_ge(S["mask_ready"], 3)
            for p in PHASES:
                with loop(act) as i:
                    (mlp if p["kind"] == MLP else attention)(p, i)

        @block.gpsimd
        def _(pool):
            pool.memset(NHALF[:, :], -0.5).then_inc(S["const_set"], 1)
            pool.memset(ONE[:, :], 0.0).then_inc(S["const_set"], 1)
            pool.memset(CM[:, :, :], 0.0).then_inc(S["const_set"], 1)
            pool.memset(EPS[:, 0, :], 1e-6).then_inc(S["const_set"], 1)
            pool.memset(EPS[:, 1, :], 1e-5).then_inc(S["const_set"], 1)
            pool.memset(VX[:, :, :, HD:VW], 1.0).then_inc(S["const_set"], 1)
            pool.wait_ge(S["const_set"], 6)
            pool.memset(ONE[0:1, :], 1.0).then_inc(S["const_set"], 1)
            for layer in range(NLAYER):
                pool.wait_ge(w_in[layer], 16)
                for at in (WQ, CQ):
                    pool.tensor_scalar(wl(layer, at), wl(layer, at), SCALE, None, ALU.mult)\
                        .then_inc(S["wq_scaled"], 1)
            pool.wait_ge(S["wrot_in"], 16)
            for n in range(0, NROT, 2):
                pool.tensor_scalar(WR[:, n * D:n * D + D], WR[:, n * D:n * D + D], SCALE, None, ALU.mult)\
                    .then_inc(S["wq_scaled"], 1)
            with loop(pool) as i:
                pool.wait_ge(S["cmoments"], i + 1)
                pool.tensor_tensor(VE[0:C, :], MV[0:C, :, 1], EPS[0:C, 0, :], ALU.add).then_inc(S["cvar"], 1)
                pool.wait_ge(S["cvar"], i + 1)
                pool.tensor_tensor(RSTD[0:C, :], VE[0:C, :], NHALF[0:C, :], ALU.pow).then_inc(S["crstd"], 1)
            pool.wait_ge(S["ct_ready"], GROUPS)
            pool.wait_ge(S["ctxt_in"], 16)

            def unit(p, i):
                n = p["n0"] + i
                pool.wait_ge(S["ln_moments"], n + 1)
                pool.tensor_tensor(VE[:, :], MV[:, :, 1], EPS[:, int(p["eps"] == 1e-5), :], ALU.add).then_inc(S["var_eps"], 1)
                pool.wait_ge(S["var_eps"], n + 1)
                pool.tensor_tensor(RSTD[:, :], VE[:, :], NHALF[:, :], ALU.pow).then_inc(S["rstd_ready"], 1)
                if p["kind"] == CROSS:
                    pool.wait_ge(S["xnt_psum"], n)
                    if p["mask"]:
                        pool.tensor_copy(CMG[:, :, :], CM[:, bass.ds(GB * i, GB), :]).then_inc(S["cm_ready"], 1)
                        pool.tensor_copy(CMTG[:, :], CMT[:, bass.ds(GB * i, GB)]).then_inc(S["cm_ready"], 1)
                    src = CTXN if p["layer"] == 0 else CTXT
                    pool.tensor_copy(CG[:, :], src[:, bass.ds(GB * C * i, GB * C)]).then_inc(S["cg_ready"], 1)
                mine = bass.ds(GB * i, GB)
                pool.wait_ge(S["yt_ready"], n + 1)
                if p["gate"] is not None:
                    pool.tensor_tensor(YT[:, :, :], YT[:, :, :], GATE[:, p["gate"], mine, :], ALU.mult)\
                        .then_inc(S["gated"], 1)
                    gated = sum(GROUPS for q in PHASES[:PHASES.index(p)] if q["gate"] is not None)
                    pool.wait_ge(S["gated"], gated + 1 + i)
                pool.tensor_tensor(X[:, mine, :], X[:, mine, :], YT[:, :, :], ALU.add).then_inc(S["x_ready"], 1)

            for p in PHASES:
                if p is PHASES[0]:
                    pool.wait_ge(S["gate_in"], 16 * NGATE)
                with loop(pool) as i:
                    unit(p, i)

        @block.vector
        def _(dve):
            dve.wait_ge(S["silu_exp"], 1)
            dve.tensor_scalar(CT[:, 1, :], CT[:, 0, :], 1.0, None, ALU.add).then_inc(S["silu_step"], 1)
            dve.wait_ge(S["silu_step"], 1)
            dve.reciprocal(CT[:, 2, :], CT[:, 1, :]).then_inc(S["silu_step"], 1)
            dve.wait_ge(S["silu_step"], 2)
            dve.tensor_tensor(CS[:, 0, :], CS[:, 1, :], CT[:, 2, :], ALU.mult).then_inc(S["cond_ready"], 1)
            dve.wait_ge(S["const_set"], 6)
            dve.wait_ge(S["small_in"], 16 * 8)
            for dst, src in ((SM[:, :], MU8[:, 0:N]), (CMT[:, :], MU8[0:C, N:N + B]),
                             (CM[0:1, :, :], CM8[:, :].rearrange("p (b c) -> p b c", b=B))):
                dve.tensor_scalar(dst, src, -1.0, BIG, ALU.add, ALU.mult).then_inc(S["mask_ready"], 1)
            for part, dst in ((0, SCL), (1, SHF)):
                dve.wait_ge(S["mod_psum"], part + 1)
                dve.tensor_tensor(dst[:, :, :], PV[:, part * 256:part * 256 + NMOD * B].rearrange("p (s b) -> p s b", b=B),
                                  MODB[:, part * NMOD:(part + 1) * NMOD].unsqueeze(2).to_broadcast([D, NMOD, B]),
                                  ALU.add).then_inc(S["mod_step"], 1)
            dve.wait_ge(S["mod_step"], 1)
            dve.tensor_scalar(SCL[:, :, :], SCL[:, :, :], 1.0, None, ALU.add).then_inc(S["mod_step"], 1)
            dve.wait_ge(S["mod_step"], 3)
            dve.tensor_tensor(SCL[:, NMOD - 3:NMOD, :], SCL[:, NMOD - 3:NMOD, :],
                              NORMW[:, :].unsqueeze(2).to_broadcast([D, 3, B]), ALU.mult).then_inc(S["mods_ready"], 1)
            dve.wait_ge(S["gatew_in"], 32)
            for k, (lo, hi) in enumerate(((0, 4 * D), (4 * D, NGATE * D))):
                dve.wait_ge(S["g_psum"], k + 1)
                dve.tensor_tensor(G[:, 1, lo:hi], SC[0:B, k, 0:hi - lo], G[:, 0, lo:hi], ALU.add)\
                   .then_inc(S["g_ready"], 1)
            for k in (0, 2, 4, 6):
                dve.tensor_scalar(COLB[:, k:k + 1], COLB[:, k:k + 1], SCALE, None, ALU.mult).then_inc(S["mask_ready"], 1)

            dve.wait_ge(S["ctx_in"], 16)
            with loop(dve) as i:
                for b in range(GB):
                    stats = dve.bn_stats(ST[0:C, b, :], CRAW[0:C, bass.ds(GB * i + b, 1), :])
                stats.then_inc(S["cstats"], 1)
                dve.wait_ge(S["cstats"], i + 1)
                dve.tensor_copy(HOLD[0:C, :], ST[0:C, 0, 0:1])
                for b in range(GB):
                    moments = dve.bn_aggr(MV[0:C, b, :], ST[0:C, b, :])
                moments.then_inc(S["cmoments"], 1)
                dve.wait_ge(S["crstd"], i + 1)
                dve.wait_ge(S["ct_psum"], i)
                for b in range(GB):
                    norm = dve.tensor_scalar(XN[0:C, b, :], CRAW[0:C, bass.ds(GB * i + b, 1), :], MV[0:C, b, 0:1],
                                             RSTD[0:C, b:b + 1], ALU.subtract, ALU.mult)
                norm.then_inc(S["cn_ready"], 1)
            dve.wait_ge(S["ct_psum"], GROUPS)

            def layer_norm(p, i):
                n = p["n0"] + i
                if p["n0"]:
                    dve.wait_ge(S["x_ready"], n - GROUPS + 1)
                for b in range(GB):
                    stats = dve.bn_stats(ST[:, b, :], X[:, bass.ds(GB * i + b, 1), :])
                stats.then_inc(S["ln_stats"], 1)
                dve.wait_ge(S["ln_stats"], n + 1)
                dve.tensor_copy(HOLD[:, :], ST[:, 0, 0:1])
                for b in range(GB):
                    moments = dve.bn_aggr(MV[:, b, :], ST[:, b, :])
                moments.then_inc(S["ln_moments"], 1)
                dve.wait_ge(S["rstd_ready"], n + 1)
                dve.wait_ge(S["xnt_psum"], n)
                for b in range(GB):
                    norm = dve.tensor_scalar(XN[:, b, :], X[:, bass.ds(GB * i + b, 1), :], MV[:, b, 0:1],
                                             RSTD[:, b:b + 1], ALU.subtract, ALU.mult)
                norm.then_inc(S["xn_ready"], 1)

            def residual(p, i):
                n = p["n0"] + i
                dve.wait_ge(S["y_psum"], n + 1)
                dve.wait_ge(S["x_ready"], n)
                y = PY[:, :].rearrange("p (b d) -> p b d", b=GB)
                if p["bias"] is None:
                    dve.tensor_copy(YT[:, :, :], y).then_inc(S["yt_ready"], 1)
                else:
                    row = ROWB[:, p["bias"]:p["bias"] + 1, :].to_broadcast([N, GB, D])
                    dve.tensor_tensor(YT[:, :, :], y, row, ALU.add).then_inc(S["yt_ready"], 1)

            def rotate(p, dst, bank, T, parts):
                v = [SC[:, k, 0:GB * T].rearrange("p (b t) -> p b t", b=GB) for k in bank]
                t = [k[:, 0:GB * T].rearrange("p (b t) -> p b t", b=GB) for k in (T1, T2)]
                for tab, k in ((RC, 0), (RS, 1)):
                    row = tab[:, p["rope"]:p["rope"] + 1, 0:T].to_broadcast([D, GB, T])
                    dve.tensor_tensor(t[k], v[k], row, ALU.mult).then_inc(S["rope_parts"], 1)
                dve.wait_ge(S["rope_parts"], parts)
                return dve.tensor_tensor(dst[:, 0:GB * T], T1[:, 0:GB * T], T2[:, 0:GB * T], ALU.add)

            def attention(p, i):
                u, T = p["u0"] + i, keys(p)
                layer_norm(p, i)
                r = p["r0"] + i
                if p["rope"] is not None:
                    dve.wait_ge(S["q_psum"], u + 1)
                    rotate(p, QT, (0, 2), N, 4 * r + 2).then_inc(S["qt_ready"], 1)
                dve.wait_ge(S["qt_ready"], u + 1)
                for j in range(2):
                    dve.tensor_scalar(QBD[:, j, :], QT[:, :], J8[:, j:j + 1], None, ALU.mult)\
                       .then_inc(S["qbd_ready"], 1)
                dve.wait_ge(S["k_psum"], u + 1)
                if p["rope"] is not None:
                    rotate(p, KT, (1, 3), T, 4 * r + 4).then_inc(S["kt_ready"], 1)
                elif p["kbias"] is None:
                    dve.tensor_copy(KT[:, 0:GB * T], SC[:, 1, 0:GB * T]).then_inc(S["kt_ready"], 1)
                else:
                    dve.tensor_scalar(KT[:, 0:GB * T], SC[:, 1, 0:GB * T], COLB[:, p["kbias"]:p["kbias"] + 1], None,
                                      ALU.add).then_inc(S["kt_ready"], 1)
                dve.wait_ge(S["v_psum"], u + 1)
                v = PV[0:T, :].rearrange("p (b h d) -> p b h d", b=GB, h=H)
                for b in range(GB):
                    if p["vbias"] is None:
                        ins = dve.tensor_copy(VX[0:T, b, :, 0:HD], v[:, b])
                    else:
                        row = ROWB[0:T, p["vbias"], :].rearrange("p (h d) -> p h d", h=H)
                        ins = dve.tensor_tensor(VX[0:T, b, :, 0:HD], v[:, b], row, ALU.add)
                ins.then_inc(S["v_ready"], 1)
                for k in range(2 * GB):
                    dve.wait_ge(S["s_psum"], 8 * u + k + 1)
                    bank = SC[:, 2 * (k % 2):2 * (k % 2) + 2, 0:HG * T].rearrange("p g (h k) -> p g h k", h=HG)
                    dve.tensor_reduce(MX[:, 8 * k:8 * k + 8].rearrange("p (g h) -> p g h", g=2), bank, AX.X, ALU.max)\
                       .then_inc(S["mx_ready"], 1)
                dve.wait_ge(S["mx_ready"], 8 * u + 8)
                dve.tensor_scalar(MHL[:, 0, :], MX[:, :], -1.0, None, ALU.mult).then_inc(S["neg_hi"], 1)
                dve.wait_ge(S["neg_hi"], u + 1)
                dve.scalar_tensor_tensor(out=MHL[:, 1, :], in0=MX[:, :], scalar=-1.0, in1=MHL[:, 0, :],
                                         op0=ALU.mult, op1=ALU.subtract).then_inc(S["neg_ready"], 1)
                dve.wait_ge(S["m_psum"], u + 1)
                dve.tensor_tensor(MBD[:, :, :], PXB.unsqueeze(1).to_broadcast([N, HG, N]),
                                  J4[:, :].unsqueeze(2).to_broadcast([N, HG, N]), ALU.mult).then_inc(S["mbd_ready"], 1)
                o = PO[:, 0:H * VW].rearrange("p (h v) -> p h v", h=H)
                for b in range(GB):
                    dve.wait_ge(S["o_psum"], 4 * u + b + 1)
                    dve.reciprocal(RDEN[:, :], o[:, :, HD]).then_inc(S["rden_ready"], 1)
                    dve.wait_ge(S["rden_ready"], 4 * u + b + 1)
                    if b >= 2:
                        dve.wait_ge(S["ot_psum"], 4 * u + b - 1)
                    dve.tensor_tensor(OQ[:, b % 2, :].rearrange("p (h d) -> p h d", h=H), o[:, :, 0:HD],
                                      RDEN[:, :].unsqueeze(2).to_broadcast([N, H, HD]), ALU.mult)\
                       .then_inc(S["oq_ready"], 1)
                residual(p, i)

            def mlp(p, i):
                layer_norm(p, i)
                residual(p, i)

            dve.wait_ge(S["const_in"], 16 * 7)
            for k in range(GROUPS):
                dve.wait_ge(x_in[k], 16)
            for p in PHASES:
                with loop(dve) as i:
                    (mlp if p["kind"] == MLP else attention)(p, i)

        @block.tensor
        def _(pe):
            def mm(o, l, r, start=True, stop=True, **more):
                return pe.matmul(o, l, r, start=start, stop=stop, **more)

            pe.wait_ge(S["cond_ready"], 1)
            for part in range(2):
                pe.wait_ge(S["mods_in"], 16 * (part + 1))
                for k in range(NMOD):
                    at = part * 256 + k * B
                    last = mm(PV[:, at:at + B], MODW[:, k * D:k * D + D], CS[:, 0 if k < 4 else 1, :])
                last.then_inc(S["mod_psum"], 1)
                pe.wait_ge(S["mod_step"], part + 1)
            pe.wait_ge(S["gatew_in"], 32)
            mm(SC[0:B, 0, 0:4 * D], CS[:, 0, :], GATEW[:, 0:4 * D]).then_inc(S["g_psum"], 1)
            mm(SC[0:B, 1, 0:3 * D], CS[:, 1, :], GATEW[:, 4 * D:7 * D]).then_inc(S["g_psum"], 1)
            pe.wait_ge(S["const_in"], 16 * 7)
            with loop(pe) as i:
                pe.wait_ge(S["cn_ready"], i + 1)
                pe.wait_ge(S["ct_ready"], i)
                for b in range(GB):
                    last = pe.transpose(PX[:, b * C:b * C + C], XN[0:C, b, :], ID[0:C, 0:C])
                last.then_inc(S["ct_psum"], 1)
            pe.wait_ge(S["ct_ready"], GROUPS)
            pe.wait_ge(S["g_ready"], 2)
            pe.wait_ge(S["const_set"], 7)

            def normed(p, i):
                n = p["n0"] + i
                pe.wait_ge(S["xn_ready"], n + 1)
                for b in range(GB):
                    last = pe.transpose(PX[:, b * N:b * N + N], XN[:, b, :], ID[:, :])
                last.then_inc(S["xnt_psum"], 1)
                pe.wait_ge(S["xnt_ready"], GB * (n + 1))

            def attention(p, i):
                u, T, layer = p["u0"] + i, keys(p), p["layer"]
                wq, wk, wv, wo = weights(p)
                normed(p, i)
                src = XNT
                if p["rope"] is not None:
                    rq, rk = ROT[p["kind"], layer]
                    mm(SC[:, 2, :], WR[:, rq:rq + D], XNT[:, :])
                mm(SC[:, 0, :], wl(layer, wq), XNT[:, :]).then_inc(S["q_psum"], 1)
                if p["kind"] == CROSS:
                    pe.wait_ge(S["cg_ready"], 4 * layer + 1 + i)
                    src = CG
                if p["rope"] is not None:
                    mm(SC[:, 3, 0:GB * T], WR[:, rk:rk + D], src[:, 0:GB * T])
                mm(SC[:, 1, 0:GB * T], wl(layer, wk), src[:, 0:GB * T]).then_inc(S["k_psum"], 1)
                for b in range(GB):
                    last = mm(PV[0:T, b * D:b * D + D], src[:, b * T:b * T + T], wl(layer, wv))
                last.then_inc(S["v_psum"], 1)

                pe.wait_ge(S["qbd_ready"], 4 * (u + 1))
                pe.wait_ge(S["kt_ready"], u + 1)
                if p["mask"] and p["kind"] == CROSS:
                    pe.wait_ge(S["cm_ready"], 2 * (i + 1))
                for k in range(2 * GB):
                    b = k // 2
                    if k >= 2:
                        pe.wait_ge(S["mx_ready"], 8 * u + k - 1)
                    for g in (2 * (k % 2), 2 * (k % 2) + 1):
                        rows = slice(32 * g, 32 * g + 32)
                        whole = SC[:, g, 0:HG * T].rearrange("p (h k) -> p h k", h=HG)
                        if p["mask"] and p["kind"] == SELF:
                            mm(whole, IDB[:, :], SM[:, :].unsqueeze(1).to_broadcast([N, HG, N]), stop=False,
                               skip_group_check=True)
                        elif p["mask"]:
                            mm(whole, ONE[:, :], CMG[:, b:b + 1, :].to_broadcast([N, HG, C]), stop=False,
                               skip_group_check=True)
                        for j in range(HG):
                            last = mm(whole[:, j, :], QBD[rows, j, b * N:b * N + N], KT[rows, b * T:b * T + T],
                                      start=not p["mask"], stop=True, skip_group_check=p["mask"])
                    last.then_inc(S["s_psum"], 1)
                pe.wait_ge(S["neg_ready"], u + 1)
                pe.transpose(PXB, MHL[:, :, :].rearrange("p a c -> p (a c)"), IDB[:, :]).then_inc(S["m_psum"], 1)

                def scores(b):
                    for pr in range(2):
                        k = 2 * b + pr
                        if k >= 2:
                            pe.wait_ge(S["p_ready"], 8 * u + k - 1)
                        for g in (2 * pr, 2 * pr + 1):
                            rows = slice(32 * g, 32 * g + 32)
                            dst = SC[0:T, g, :].rearrange("p (h q) -> p h q", h=HG)
                            masked = p["mask"] and p["kind"] == SELF
                            if masked:
                                mm(dst, SM[:, :], IDB[:, :].unsqueeze(1).to_broadcast([N, HG, N]), stop=False)
                            mm(dst, KT[rows, b * T:b * T + T], QBD[rows, :, b * N:b * N + N], start=not masked,
                               stop=False)
                            last = mm(dst, SEL[:, NHG * b + g, 0:T], MBD[:, :, :], start=False)
                        last.then_inc(S["st_psum"], 1)

                def values(b):
                    pe.wait_ge(S["p_ready"], 8 * u + 2 * b + 2)
                    if b:
                        pe.wait_ge(S["oq_ready"], 4 * u + b)
                    for h in range(H):
                        last = mm(PO[:, h * VW:h * VW + VW], PR[0:T, b % 2, h * N:h * N + N], VX[0:T, b, h, :])
                    last.then_inc(S["o_psum"], 1)

                def project(b):
                    pe.wait_ge(S["oq_ready"], 4 * u + b + 1)
                    pe.transpose(PX[:, 0:N], OQ[:, b % 2, :], ID[:, :]).then_inc(S["ot_psum"], 1)
                    pe.wait_ge(S["ot_ready"], 4 * u + b + 1)
                    last = mm(PY[:, b * D:b * D + D], OT[:, b, :], wl(layer, wo))
                    if b == GB - 1:
                        last.then_inc(S["y_psum"], 1)

                pe.wait_ge(S["mbd_ready"], u + 1)
                pe.wait_ge(S["v_ready"], u + 1)
                pe.wait_ge(S["yt_ready"], p["n0"] + i)
                for b in range(GB + 2):
                    if b < GB:
                        scores(b)
                    if b >= 2:
                        project(b - 2)
                    if 1 <= b <= GB:
                        values(b - 1)

            def mlp(p, i):
                m, layer = p["m0"] + i, p["layer"]
                normed(p, i)
                for c in range(FF // D):
                    mm(SC[:, c, :], wl(layer, W1 + c * D), XNT[:, :]).then_inc(S["h_psum"], 1)
                pe.wait_ge(S["yt_ready"], p["n0"] + i)
                pe.wait_ge(S["h_ready"], 4 * (m + 1))
                for b in range(GB):
                    for c in range(FF // D):
                        last = mm(PY[:, b * D:b * D + D], HT[:, c, b * N:b * N + N], wl(layer, W2 + c * D),
                                  start=c == 0, stop=c == FF // D - 1)
                last.then_inc(S["y_psum"], 1)

            for p in PHASES:
                if p["kind"] == SELF:
                    pe.wait_ge(w_in[p["layer"]], 16)
                    pe.wait_ge(S["wq_scaled"], 2 * p["layer"] + 2 if p["layer"] < 2 else 2 * NLAYER + NROT // 2)
                with loop(pe) as i:
                    (mlp if p["kind"] == MLP else attention)(p, i)


def kernel(**inputs):
    import ml_dtypes
    import concourse.bacc as bacc
    from concourse.bass_utils import run_bass_kernel_spmd

    t = {k: np.asarray(v) for k, v in inputs.items()}
    L = [{k[9:]: v for k, v in t.items() if k.startswith(f"L{n}_xcond_")} for n in range(4)]
    a, b, c, d = L

    def rows(wt):
        return np.concatenate([wt[k * D:k * D + D] for k in range(FF // D)], axis=1)

    qkv2 = c["qkv_w"].T
    layers = [
        [a["W_qkv"], a["W_proj"], a["W_qc"], a["W_kvc"], a["W_cproj"], a["W_mlp1"], rows(a["W_mlp2"])],
        [b["qkv_w"], b["sa_proj_w"], b["q_w"], b["kv_w"], b["ca_proj_w"], b["fc1_w"], rows(b["fc2_w"])],
        [qkv2, c["sa_out_w"].T, c["q_w"].T, c["k_w"].T, c["v_w"].T, c["ca_out_w"].T, c["ffn_w1"].T,
         rows(c["ffn_w2"].T)],
        [d["qkv_W"], d["attn_out_W"], d["cq_W"], d["ck_W"], d["cv_W"], d["co_W"], d["mlp_W1"], rows(d["mlp_W2"])],
    ]
    w = np.stack([np.concatenate(x, axis=1) for x in layers])
    swap = np.arange(D).reshape(H, 2, HD // 2)[:, ::-1].reshape(-1)
    wrot = np.concatenate([qkv2[:, :D][:, swap], qkv2[:, D:2 * D][:, swap], c["q_w"].T[:, swap], c["k_w"].T[:, swap],
                           d["qkv_W"][:, :D][:, swap], d["qkv_W"][:, D:2 * D][:, swap]], axis=1)

    def cut(m, n):
        return m[..., n * D:(n + 1) * D]

    lns = [(c[f"ln{k}_w"].T, c[f"ln{k}_b"]) for k in (1, 2, 3)]
    scale = [(a["W_mod"], a["b_mod"], 1), (a["W_mod"], a["b_mod"], 4), (b["adaln_w"], b["adaln_b"], 1),
             (b["adaln_w"], b["adaln_b"], 4)] + [(x, y, 0) for x, y in lns] + \
            [(d["adaLN_W"], d["adaLN_b"], k) for k in (1, 4, 7)]
    shift = [(a["W_mod"], a["b_mod"], 0), (a["W_mod"], a["b_mod"], 3), (b["adaln_w"], b["adaln_b"], 0),
             (b["adaln_w"], b["adaln_b"], 3)] + [(x, y, 1) for x, y in lns] + \
            [(d["adaLN_W"], d["adaLN_b"], k) for k in (0, 3, 6)]
    gate = [(a["W_mod"], a["b_mod"], 2), (a["W_mod"], a["b_mod"], 5), (b["adaln_w"], b["adaln_b"], 2),
            (b["adaln_w"], b["adaln_b"], 5)] + [(d["adaLN_W"], d["adaLN_b"], k) for k in (2, 5, 8)]
    modw = np.concatenate([cut(x, n) for x, _, n in scale + shift], axis=1)
    modb = np.stack([cut(y, n) for _, y, n in scale + shift], axis=1)
    gatew = np.concatenate([cut(x, n) for x, _, n in gate], axis=1)
    gateb = np.concatenate([cut(y, n) for _, y, n in gate])
    colb = np.stack([cut(a["b_qkv"], 0), cut(a["b_qkv"], 1), a["b_qc"], cut(a["b_kvc"], 0),
                     cut(b["qkv_b"], 0), cut(b["qkv_b"], 1), b["q_b"], cut(b["kv_b"], 0)], axis=1)
    rowb = np.stack([a["b_proj"], a["b_cproj"], a["b_mlp2"], b["sa_proj_b"], b["ca_proj_b"], b["fc2_b"],
                     c["ffn_b2"], d["mlp_b2"], cut(a["b_qkv"], 2), cut(a["b_kvc"], 1), cut(b["qkv_b"], 2),
                     cut(b["kv_b"], 1)])
    mlpb = np.stack([x.reshape(FF // D, D).T for x in (a["b_mlp1"], b["fc1_b"], c["ffn_b1"], d["mlp_b1"])], axis=1)

    row = np.arange(D)
    jmask8 = (row[:, None] % 32 // HD == np.arange(HG)).astype(np.float32)
    jmask4 = (row[:, None] % HG == np.arange(HG)).astype(np.float32)
    sel = np.repeat((row[:, None] % 64 // HG == np.arange(GB * NHG))[:, :, None], N, axis=2).astype(ml_dtypes.bfloat16)
    half = HD // 2
    freq = (1.0 / 10000.0 ** (np.arange(half, dtype=np.float32) / half)).astype(np.float32)[row % half]
    pos = np.stack([np.arange(N), np.arange(N) % (N // 2)]).astype(np.float32)
    ang = freq[:, None, None] * pos[None]
    sign = np.where(row % HD < half, -1.0, 1.0).astype(np.float32)[:, None, None]
    arrays = dict(
        x=t["x"], cond_t=t["cond_1024"].T, ctx_tok=t["ctx_1024"], ctx_t=t["ctx_1024"].reshape(B * C, D).T,
        w=w, wrot=wrot, modw=modw, modb=modb, gatew=gatew, gateb=gateb,
        normw=np.stack([d["norm1_w"], d["normc_w"], d["norm2_w"]], axis=1), colb=colb, rowb=rowb, mlpb=mlpb,
        smask=t["mask_SxS_bk0"], cmask=t["mask_BxS2_bf1"].reshape(1, B * C),
        cmask_t=t["mask_BxS2_bf1"].T,
        ident=np.eye(N, dtype=np.float32), identb=np.eye(N, dtype=np.float32).astype(ml_dtypes.bfloat16),
        jmask8=jmask8, jmask4=jmask4, sel=sel,
        ropec=np.cos(ang).astype(np.float32), ropes=(np.sin(ang) * sign).astype(np.float32))
    arrays = {"in_" + k: np.ascontiguousarray(v) for k, v in arrays.items()}
    nc = bacc.Bacc("TRN2", target_bir_lowering=False, num_devices=1)
    args = {k[3:]: nc.dram_tensor(k, v.shape, mybir.dt.from_np(v.dtype), kind="ExternalInput").ap()
            for k, v in arrays.items()}
    out = nc.dram_tensor("out", (B, N, D), F32, kind="ExternalOutput").ap()
    build(nc, out=out, **args)
    r = run_bass_kernel_spmd(nc, [arrays], core_ids=[0])
    return r.results[0]["out"]
```

```python
from contextlib import ExitStack

import numpy as np

import concourse.bass as bass
from concourse import mybir

ALU = mybir.AluOpType
ACT = mybir.ActivationFunctionType
AX = mybir.AxisListType
F32 = mybir.dt.float32
BF16 = mybir.dt.bfloat16
U8 = mybir.dt.uint8

B, N, D = 16, 128, 128
H, HD = 16, 8
C = 77
FF = 512
NC = FF // D
GB = 2
GROUPS = B // GB
TOK = GB * N
HG = 4
NHG = H // HG
PARTS = 3
KPARTS = (0, 0, 0, 1, 1, 2)
VT, VW = 6, 32
ONE_AT = 24
TILE_HEADS = [[0, 1, 2], [3, 4, 5], [6, 7, 8], [9, 10, 11], [12, 13], [14, 15]]
OUT_HEADS = [TILE_HEADS[t][k] for k in range(3) for t in range(4)] + [12, 14, 13, 15]
SCALE = float(HD) ** -0.5
BIG = 3.3895313892515355e38

SELF, CROSS, MLP = range(3)


def phase(kind, layer, **more):
    p = dict(kind=kind, layer=layer, mod=None, gate=None, bias=None, qk=None, rope=None, mask=False, eps=0,
             gelu=None)
    p.update(more)
    return p


PHASES = [
    phase(SELF, 0, mod=0, gate=0, bias=0, qk=0),
    phase(CROSS, 0, bias=1, qk=2),
    phase(MLP, 0, mod=1, gate=1, bias=2, gelu="tanh"),
    phase(SELF, 1, mod=2, gate=2, bias=3, qk=4),
    phase(CROSS, 1, bias=4, qk=6),
    phase(MLP, 1, mod=3, gate=3, bias=5, gelu="tanh"),
    phase(SELF, 2, mod=4, rope=0, eps=1),
    phase(CROSS, 2, mod=5, rope=1, eps=1),
    phase(MLP, 2, mod=6, bias=6, eps=1, gelu="erf"),
    phase(SELF, 3, mod=7, gate=4, rope=2, mask=True, eps=1),
    phase(CROSS, 3, mod=8, gate=5, mask=True, eps=1),
    phase(MLP, 3, mod=9, gate=6, bias=7, eps=1, gelu="tanh"),
]
NMOD, NGATE, NBIAS, NLAYER, NROPE = 10, 7, 8, 4, 3
NEXT = dict(unit=0, att=0, mlp=0, rope=0, gated=0, cross=0)
for p_ in PHASES:
    p_.update({k + "0": v for k, v in NEXT.items()})
    NEXT["unit"] += GROUPS
    NEXT["att"] += GROUPS * (p_["kind"] != MLP)
    NEXT["mlp"] += GROUPS * (p_["kind"] == MLP)
    NEXT["rope"] += GROUPS * (p_["rope"] is not None)
    NEXT["gated"] += GROUPS * (p_["gate"] is not None)
    NEXT["cross"] += GROUPS * (p_["kind"] == CROSS)


class Unit:

    def __init__(self, p, i, parity):
        self.p, self.i, self.par = p, i, parity
        self.kind, self.layer = p["kind"], p["layer"]
        self.T = N if self.kind == SELF else C
        self.attends = self.kind != MLP

    def n(self, sort="unit"):
        return self.p[sort + "0"] + self.i

    def seq(self, b=0):
        return GB * self.i + b


def static(n):
    if 0 <= n < GROUPS * len(PHASES):
        return Unit(PHASES[n // GROUPS], n % GROUPS, n % 2)
    return None


def run(eng, unit):
    for k, p in enumerate(PHASES):
        first = GROUPS * k

        def alone(n):
            unit(*[static(m) for m in (n - 1, n, n + 1, n + 2)])

        alone(first)
        alone(first + 1)
        with eng.Fori(1, GROUPS // 2 - 1) as pair:
            for odd in range(2):
                unit(*[Unit(p, pair * 2 + (odd + m), (odd + m) % 2) for m in (-1, 0, 1, 2)])
        alone(first + GROUPS - 2)
        alone(first + GROUPS - 1)


VC = VT * VW
WQ, WK, WV, WO, CQ, CK, CV, CO, W1, W2, WEND = np.cumsum([0, D, D, VC, D, D, D, VC, D, FF, FF]).tolist()

def build(nc, x, cond_t, ctx_tok, ctx_t, w, wrot, modw, modb, gatew, gateb, normw, colb, rowb, rowv, mlpb,
          smask, cmask, cmask_t, ident, identb, jmask4, sel, ropec, ropes, out):
    with ExitStack() as ctx:
        def sb(name, shape, dt=F32):
            return ctx.enter_context(nc.sbuf_tensor(name, shape, dt))

        X = sb("X", [N, B, D])
        W = sb("W", [D, NLAYER, WEND])
        WR = sb("WR", [D, NROPE, 2, D])
        SCL = sb("SCL", [D, NMOD, B])
        SHF = sb("SHF", [D, NMOD, B])
        CTXT = sb("CTXT", [D, B * C])
        CTXN = sb("CTXN", [D, B * C])
        COLB = sb("COLB", [D, 8])
        ROWB = sb("ROWB", [N, NBIAS, D])
        ROWV = sb("ROWV", [N, 8, VC])
        MLPB = sb("MLPB", [D, NLAYER, NC])
        ID = sb("ID", [N, N])
        IDB = sb("IDB", [N, N], BF16)
        J4 = sb("J4", [N, HG])
        SEL = sb("SEL", [N, GB * NHG, N], BF16)
        RC = sb("RC", [D, NROPE, 2 * TOK])
        RS = sb("RS", [D, NROPE, 2 * TOK])
        SM = sb("SM", [N, N], BF16)
        CM = sb("CM", [N, B, C], BF16)
        CMT = sb("CMT", [C, B])
        ONE = sb("ONE", [N, N], BF16)
        NHALF = sb("NHALF", [N, GB])
        EPS = sb("EPS", [N, 2, GB])
        XN = sb("XN", [N, GB, D])
        ST = sb("STAT", [N, GB, 6])
        HOLD = sb("HOLD", [N, 1])
        HELD = sb("HELD", [N, 1])
        MV = sb("MV", [N, GB, 2])
        VE = sb("VE", [N, GB])
        RSTD = sb("RSTD", [N, GB])
        XNT = sb("XNT", [D, 2, TOK])
        GATE = sb("GATE", [N, 2, GB, D])
        CG = sb("CG", [D, 2, GB * C])
        CMG = sb("CMG", [N, 2, GB, C], BF16)
        CMTG = sb("CMTG", [C, 2, GB])
        WORK = sb("WORK", [D, 4, 2 * TOK])
        QKT, T1, T2, R1 = [WORK[:, k, :] for k in range(4)]
        PT = sb("PT", [D, PARTS, 2 * TOK], BF16)
        QH = sb("QH", [N, 2, H, TOK], BF16)
        KH = sb("KH", [N, 2, H * TOK], BF16)
        VX = sb("VX", [N, 2, GB, VC])
        VXC = sb("VXC", [N, 2, GB, VC])
        MX = sb("MX", [N, GB * H])
        MHL = sb("MHL", [N, 2, N // 2], BF16)
        MBD = sb("MBD", [N, HG, N], BF16)
        PR = sb("PR", [N, GB, H * N])
        HT = sb("HT", [D, NC, TOK])
        OSA = sb("OSA", [N, GB, 3 * N])
        OSB = sb("OSB", [N // 2, GB, 2 * N])
        RDEN = sb("RDEN", [N, H])
        OQ = sb("OQ", [N, GB, D])
        OT = sb("OT", [D, GB, N])
        YT = sb("YT", [N, GB, D])
        CRAW = PR[:, 0, :].rearrange("p (b d) -> p b d", b=B)
        MODW = PR[:, 1, :]
        GATEW = HT[:, :, :].rearrange("p c t -> p (c t)")[:, 0:NGATE * D]
        G = WORK[0:B, :, :].rearrange("p a t -> p (a t)")[:, 0:2 * NGATE * D].rearrange("p (a c) -> p a c", a=2)
        CS = sb("CS", [D, 2, B])
        CT = sb("CT", [D, 3, B])
        MODB = sb("MODB", [D, 2 * NMOD])
        NORMW = sb("NORMW", [D, 3])
        MU8 = sb("MU8", [N, N + B], U8)
        CM8 = sb("CM8", [1, B * C], U8)
        gate_dram = nc.dram_tensor("gate_rows", (B, NGATE * D), F32, kind="Internal").ap()
        q_dram = nc.dram_tensor("q_parts", (2, PARTS, D, TOK), BF16, kind="Internal").ap()
        ks_dram = nc.dram_tensor("k_parts", (2, PARTS, D, TOK), BF16, kind="Internal").ap()
        kc_dram = nc.dram_tensor("k_context_parts", (2, PARTS, D, GB * C), BF16, kind="Internal").ap()

        SC = ctx.enter_context(nc.psum_tensor("SC", [N, 4, 512], F32))
        POA = ctx.enter_context(nc.psum_tensor("POA", [N, 512], F32))
        POB = ctx.enter_context(nc.psum_tensor("POB", [N, 512], F32))
        TP = ctx.enter_context(nc.psum_tensor("TP", [N, 2, 512], F32))
        TR, PY = TP[:, 0, :], TP[:, 1, :]
        PYOT = PY[:, 2 * D:3 * D]
        PYM = PY[:, 3 * D:3 * D + N // 2].bitcast(BF16)
        flat = TP[:, :, :].rearrange("p a c -> p (a c)")
        own_a = flat[:, 0:3 * (N + HD)].rearrange("p (i s) -> p i s", s=N + HD)[:, :, 0:N]\
            .rearrange("p i (t c) -> p i t c", c=VW)[:, :, :, 0:HD]
        own_b = flat[:, 3 * N:3 * N + 2 * (N // 2 + HD)].rearrange("p (i s) -> p i s", s=N // 2 + HD)[:, :, 0:N // 2]\
            .rearrange("p i (t c) -> p i t c", c=VW)[:, :, :, 0:HD]
        sums = TR.rearrange("p (n c) -> p n c", c=VW)[:, :, ONE_AT]

        names = ("cond_in mods_in gatew_in small_in ctx_in ctxt_in const_in wrot_in gate_out gate_in out_done "
                 "silu_exp silu_step cond_ready mod_psum mod_step mods_ready g_psum g_ready mask_ready const_set "
                 "wq_scaled cstats cmoments cvar crstd cn_ready ct_psum ct_ready "
                 "ln_stats ln_moments var_eps rstd_ready xn_ready xnt_psum xnt_ready cg_ready cm_ready "
                 "qk_psum v_psum rope_parts qkt_ready part1 rest1 part2 part3 parts_out qk_in v_ready "
                 "s_psum mx_ready neg_hi neg_ready m_psum mbd_ready st_psum p_ready o_psum oa_ready ob_ready "
                 "tr_psum rden_ready oq_ready ot_psum ot_ready y_psum yt_ready gated x_ready h_psum h_ready").split()
        S = {k: ctx.enter_context(nc.semaphore("s_" + k)) for k in names}
        x_in = [ctx.enter_context(nc.semaphore(f"s_x_in{i}")) for i in range(4)]
        w_in = [ctx.enter_context(nc.semaphore(f"s_w_in{i}")) for i in range(NLAYER)]
        block = ctx.enter_context(nc.Block())
        NCONST, NSMALL = 6, 9

        def wait(eng, name, value):
            if not isinstance(value, int) or value > 0:
                eng.wait_ge(S[name], value)

        def wl(layer, at, width=D):
            return W[:, layer, at:at + width]

        def weights(u):
            return (WQ, WK, WV, WO) if u.kind == SELF else (CQ, CK, CV, CO)

        def width(u):
            return TOK + GB * u.T

        def k_dram(u):
            return ks_dram if u.kind == SELF else kc_dram

        @block.sync
        def _(sp):
            sp.dma_start(CS[:, 1, :], cond_t).then_inc(S["cond_in"], 16)
            for k in range(4):
                sp.dma_start(X[:, 4 * k:4 * k + 4, :],
                             x[4 * k:4 * k + 4].rearrange("b t d -> t b d")).then_inc(x_in[k], 16)
                if k == 0:
                    sp.dma_start(W[:, 0, :], w[0]).then_inc(w_in[0], 16)
                    sp.dma_start(CRAW[0:C, :, :], ctx_tok.rearrange("b c d -> c b d")).then_inc(S["ctx_in"], 16)
            sp.wait_ge(S["g_ready"], 2)
            sp.dma_start(gate_dram, G[:, 1, :]).then_inc(S["gate_out"], 16)
            sp.wait_ge(S["gate_out"], 16)
            sp.wait_ge(S["const_set"], 8)

            def ahead(*values):
                return [v if isinstance(v, int) else sp.to_reg(v) for v in values]

            def stack(u):
                a = u.n("att")
                loaded, split, left, used = ahead(144 * a, a + 1, 32 * (a + 1), 4 * (a - 1))
                wait(sp, "qk_in", loaded)
                wait(sp, "part3", split)
                wait(sp, "st_psum", used)
                sp.dma_start(q_dram[u.par].rearrange("x r t -> r x t"), PT[:, :, 0:TOK]).then_inc(S["parts_out"], 16)
                sp.dma_start(k_dram(u)[u.par].rearrange("x r t -> r x t"), PT[:, :, TOK:width(u)])\
                  .then_inc(S["parts_out"], 16)
                wait(sp, "parts_out", left)
                row = 0
                for n in (3, 2, 1):
                    sp.dma_start(QH[row:row + HD * n, u.par, :, :].rearrange("r h t -> r (h t)"),
                                 q_dram[u.par, 0:n].rearrange("x (d h) t -> (x d) (h t)", d=HD)).then_inc(S["qk_in"], 16)
                    row += HD * n
                for k, part in enumerate(KPARTS):
                    sp.dma_start(KH[HD * k:HD * k + HD, u.par, 0:H * GB * u.T],
                                 k_dram(u)[u.par, part].rearrange("(d h) t -> d (h t)", d=HD)).then_inc(S["qk_in"], 16)

            def gates(u):
                if u.p["gate"] is not None:
                    used, last = ahead(u.n() - 1, 16 * u.n("gated"))
                    wait(sp, "x_ready", used)
                    wait(sp, "gate_in", last)
                    at = u.p["gate"] * D
                    sp.dma_start(GATE[:, u.par, :, :],
                                 gate_dram[bass.ds(u.seq(), GB), at:at + D].partition_broadcast(N))\
                      .then_inc(S["gate_in"], 16)

            def unit(prev, u, nxt, nxt2):
                if nxt and nxt.attends:
                    stack(nxt)
                if nxt:
                    gates(nxt)
                if u.p is PHASES[-1]:
                    wait(sp, "x_ready", *ahead(u.n() + 1))
                    sp.dma_start(out[bass.ds(u.seq(), GB)].rearrange("b t d -> t b d"),
                                 X[:, bass.ds(u.seq(), GB), :]).then_inc(S["out_done"], 16)

            stack(static(0))
            for layer in range(1, NLAYER):
                sp.dma_start(W[:, layer, :], w[layer]).then_inc(w_in[layer], 16)
            sp.dma_start(WR[:, :, :, :], wrot).then_inc(S["wrot_in"], 16)
            sp.dma_start(CTXT[:, :], ctx_t).then_inc(S["ctxt_in"], 16)
            gates(static(0))
            run(sp, unit)
            sp.wait_ge(S["out_done"], 16 * GROUPS)

        @block.scalar
        def _(act):
            for dst, src in ((ID[:, :], ident), (IDB[:, :], identb), (J4[:, :], jmask4),
                             (SEL[:, :, :], sel), (RC[:, :, :], ropec), (RS[:, :, :], ropes)):
                act.dma_start(dst, src).then_inc(S["const_in"], 16)
            act.dma_start(MODB[:, :], modb).then_inc(S["small_in"], 16)
            act.dma_start(NORMW[:, :], normw).then_inc(S["small_in"], 16)
            act.dma_start(COLB[:, :], colb).then_inc(S["small_in"], 16)
            act.dma_start(MLPB[:, :, :], mlpb).then_inc(S["small_in"], 16)
            act.dma_start(ROWB[:, :, :], rowb.partition_broadcast(N)).then_inc(S["small_in"], 16)
            act.dma_start(ROWV[:, :, :], rowv.partition_broadcast(N)).then_inc(S["small_in"], 16)
            act.dma_start(MU8[:, 0:N], smask).then_inc(S["small_in"], 16)
            act.dma_start(MU8[0:C, N:N + B], cmask_t).then_inc(S["small_in"], 16)
            act.dma_start(CM8[:, :], cmask).then_inc(S["small_in"], 16)
            act.dma_start(GATEW, gatew).then_inc(S["gatew_in"], 16)
            act.dma_start(G[:, 0, :], gateb.partition_broadcast(B)).then_inc(S["gatew_in"], 16)
            act.wait_ge(S["cond_in"], 16)
            act.activation(CT[:, 0, :], CS[:, 1, :], ACT.Exp, scale=-1.0).then_inc(S["silu_exp"], 1)
            for part in range(2):
                if part:
                    act.wait_ge(S["mod_psum"], 1)
                act.dma_start(MODW[:, 0:NMOD * D], modw[:, part * NMOD * D:(part + 1) * NMOD * D])\
                   .then_inc(S["mods_in"], 16)

            act.wait_ge(S["ct_psum"], 1)
            with act.Fori(0, GROUPS) as i:
                act.wait_ge(S["ct_psum"], i + 1)
                act.activation(CTXN[:, bass.ds(GB * C * i, GB * C)], TR[:, 0:GB * C], ACT.Copy)\
                   .then_inc(S["ct_ready"], 1)

            def normed(u):
                wait(act, "xnt_psum", u.n() + 1)
                m = u.p["mod"]
                if m is None:
                    act.activation(XNT[:, u.par, :], TR[:, 0:TOK], ACT.Copy).then_inc(S["xnt_ready"], GB)
                    return
                for b in range(GB):
                    s = bass.ds(u.seq(b), 1)
                    act.activation(XNT[:, u.par, b * N:b * N + N], TR[:, b * N:b * N + N], ACT.Identity,
                                   bias=SHF[:, m, s], scale=SCL[:, m, s]).then_inc(S["xnt_ready"], 1)

            def qk(u):
                a, end = u.n("att"), width(u)
                if u.p["rope"] is None:
                    wait(act, "qk_psum", a + 1)
                    if u.p["qk"] is None:
                        act.activation(QKT[:, 0:end], POB[:, 0:end], ACT.Copy).then_inc(S["qkt_ready"], 2)
                    else:
                        for k, (lo, hi) in enumerate(((0, TOK), (TOK, end))):
                            c = u.p["qk"] + k
                            act.activation(QKT[:, lo:hi], POB[:, lo:hi], ACT.Identity, bias=COLB[:, c:c + 1])\
                               .then_inc(S["qkt_ready"], 1)
                wait(act, "parts_out", 32 * a)
                wait(act, "qkt_ready", 2 * (a + 1))
                act.activation(PT[:, 0, 0:end], QKT[:, 0:end], ACT.Copy).then_inc(S["part1"], 1)

            def transposed(u, b):
                wait(act, "ot_psum", 2 * u.n("att") + b + 1)
                act.activation(OT[:, b, :], PYOT, ACT.Copy).then_inc(S["ot_ready"], 1)

            def probabilities(u, k):
                b, pr = divmod(k, 2)
                more = {}
                if u.p["mask"] and u.kind == CROSS:
                    more = dict(bias=CMTG[:, u.par, b:b + 1])
                wait(act, "st_psum", 4 * u.n("att") + k + 1)
                act.activation(PR[0:u.T, b, pr * 1024:pr * 1024 + 1024], SC[0:u.T, 2 * pr:2 * pr + 2, :],
                               ACT.Exp, **more).then_inc(S["p_ready"], 1)

            def outputs(u, b):
                wait(act, "o_psum", 2 * u.n("att") + b + 1)
                act.activation(OSA[:, b, :], POA[:, 0:3 * N], ACT.Copy).then_inc(S["oa_ready"], 1)

            def unit(prev, u, nxt, nxt2):
                if prev and prev.attends:
                    transposed(prev, 1)
                if not u.attends:
                    f = ACT.Gelu if u.p["gelu"] == "erf" else ACT.Gelu_apprx_tanh
                    for c in range(NC):
                        wait(act, "h_psum", NC * u.n("mlp") + c + 1)
                        act.activation(HT[:, c, :], SC[:, c, 0:TOK], f,
                                       bias=MLPB[:, u.layer, c:c + 1]).then_inc(S["h_ready"], 1)
                if nxt and nxt.attends:
                    qk(nxt)
                if nxt2:
                    normed(nxt2)
                if u.attends:
                    if u.p["mask"] and u.kind == CROSS:
                        wait(act, "cm_ready", 2 * (u.i + 1))
                    for k in range(3):
                        probabilities(u, k)
                    outputs(u, 0)
                    probabilities(u, 3)
                    transposed(u, 0)
                    outputs(u, 1)

            act.wait_ge(S["mods_ready"], 1)
            act.wait_ge(S["const_in"], 16 * NCONST)
            act.wait_ge(S["mask_ready"], 7)
            act.wait_ge(S["gate_out"], 16)
            normed(static(0))
            normed(static(1))
            qk(static(0))
            run(act, unit)

        @block.gpsimd
        def _(pool):
            def hold():
                pool.tensor_tensor(HELD[:, :], NHALF[:, 0:1], NHALF[:, 0:1], ALU.mult)

            pool.memset(NHALF[:, :], -0.5).then_inc(S["const_set"], 1)
            pool.memset(EPS[:, 0, :], 1e-6).then_inc(S["const_set"], 1)
            pool.memset(EPS[:, 1, :], 1e-5).then_inc(S["const_set"], 1)
            pool.memset(ONE[:, :], 0.0).then_inc(S["const_set"], 1)
            pool.memset(CM[:, :, :], 0.0).then_inc(S["const_set"], 1)
            pool.wait_ge(S["const_set"], 5)
            pool.memset(ONE[0:1, :], 1.0).then_inc(S["const_set"], 1)
            pool.wait_ge(w_in[0], 16)
            for at in (WQ, CQ):
                pool.tensor_scalar(wl(0, at), wl(0, at), SCALE, None, ALU.mult).then_inc(S["wq_scaled"], 1)
            pool.memset(QH[:, :, :, :], 0.0).then_inc(S["const_set"], 1)
            pool.memset(KH[:, :, :], 0.0).then_inc(S["const_set"], 1)
            pool.memset(VXC[:, :, :, :], 0.0).then_inc(S["const_set"], 1)
            pool.memset(MHL[:, :, :], 0.0).then_inc(S["const_set"], 1)
            with pool.Fori(0, GROUPS) as i:
                pool.wait_ge(S["cmoments"], i + 1)
                pool.tensor_tensor(VE[0:C, :], MV[0:C, :, 1], EPS[0:C, 0, :], ALU.add).then_inc(S["cvar"], 1)
                pool.wait_ge(S["cvar"], i + 1)
                pool.tensor_tensor(RSTD[0:C, :], VE[0:C, :], NHALF[0:C, :], ALU.pow).then_inc(S["crstd"], 1)

            def moments(u):
                n = u.n()
                wait(pool, "ln_moments", n + 1)
                pool.tensor_tensor(VE[:, :], MV[:, :, 1], EPS[:, u.p["eps"], :], ALU.add).then_inc(S["var_eps"], 1)
                wait(pool, "var_eps", n + 1)
                pool.tensor_tensor(RSTD[:, :], VE[:, :], NHALF[:, :], ALU.pow).then_inc(S["rstd_ready"], 1)
                if u.kind == CROSS:
                    src = CTXN if u.layer == 0 else CTXT
                    pool.tensor_copy(CG[:, u.par, :], src[:, bass.ds(C * u.seq(), GB * C)]).then_inc(S["cg_ready"], 1)

            def parts(u):
                a, end = u.n("att"), width(u)
                wait(pool, "rest1", a + 1)
                wait(pool, "parts_out", 32 * a)
                hold()
                pool.tensor_copy(PT[:, 1, 0:end], R1[:, 0:end]).then_inc(S["part2"], 1)
                wait(pool, "part2", a + 1)
                pool.tensor_tensor(PT[:, 2, 0:end], R1[:, 0:end], PT[:, 1, 0:end], ALU.subtract)\
                    .then_inc(S["part3"], 1)
                if u.kind == CROSS and u.p["mask"]:
                    wait(pool, "p_ready", 4 * (a - 1))
                    hold()
                    pool.tensor_copy(CMG[:, u.par, :, :], CM[:, bass.ds(u.seq(), GB), :]).then_inc(S["cm_ready"], 1)
                    pool.tensor_copy(CMTG[:, u.par, :], CMT[:, bass.ds(u.seq(), GB)]).then_inc(S["cm_ready"], 1)

            def add(u):
                mine = bass.ds(u.seq(), GB)
                wait(pool, "yt_ready", u.n() + 1)
                if u.p["gate"] is not None:
                    wait(pool, "gate_in", 16 * (u.n("gated") + 1))
                    pool.tensor_tensor(YT[:, :, :], YT[:, :, :], GATE[:, u.par, :, :], ALU.mult)\
                        .then_inc(S["gated"], 1)
                    wait(pool, "gated", u.n("gated") + 1)
                pool.tensor_tensor(X[:, mine, :], X[:, mine, :], YT[:, :, :], ALU.add).then_inc(S["x_ready"], 1)

            def unit(prev, u, nxt, nxt2):
                if nxt2:
                    moments(nxt2)
                if nxt and nxt.attends:
                    parts(nxt)
                if prev:
                    add(prev)

            moments(static(0))
            moments(static(1))
            parts(static(0))
            for layer in range(1, NLAYER):
                pool.wait_ge(w_in[layer], 16)
                for at in (WQ, CQ):
                    pool.tensor_scalar(wl(layer, at), wl(layer, at), SCALE, None, ALU.mult)\
                        .then_inc(S["wq_scaled"], 1)
            pool.wait_ge(S["wrot_in"], 16)
            for k in range(NROPE):
                pool.tensor_scalar(WR[:, k, 0, :], WR[:, k, 0, :], SCALE, None, ALU.mult)\
                    .then_inc(S["wq_scaled"], 1)
            pool.wait_ge(S["ct_ready"], GROUPS)
            pool.wait_ge(S["ctxt_in"], 16)
            pool.wait_ge(S["mask_ready"], 3)
            run(pool, unit)
            add(static(GROUPS * len(PHASES) - 1))

        @block.vector
        def _(dve):
            dve.wait_ge(S["silu_exp"], 1)
            dve.tensor_scalar(CT[:, 1, :], CT[:, 0, :], 1.0, None, ALU.add).then_inc(S["silu_step"], 1)
            dve.wait_ge(S["silu_step"], 1)
            dve.reciprocal(CT[:, 2, :], CT[:, 1, :]).then_inc(S["silu_step"], 1)
            dve.wait_ge(S["silu_step"], 2)
            dve.tensor_tensor(CS[:, 0, :], CS[:, 1, :], CT[:, 2, :], ALU.mult).then_inc(S["cond_ready"], 1)
            dve.wait_ge(S["small_in"], 16 * NSMALL)
            dve.wait_ge(S["const_set"], 5)
            for dst, src in ((SM[:, :], MU8[:, 0:N]), (CMT[:, :], MU8[0:C, N:N + B]),
                             (CM[0:1, :, :], CM8[:, :].rearrange("p (b c) -> p b c", b=B))):
                dve.tensor_scalar(dst, src, -1.0, BIG, ALU.add, ALU.mult).then_inc(S["mask_ready"], 1)
            for part, dst in ((0, SCL), (1, SHF)):
                dve.wait_ge(S["mod_psum"], part + 1)
                dve.tensor_tensor(dst[:, :, :],
                                  PY[:, part * 256:part * 256 + NMOD * B].rearrange("p (s b) -> p s b", b=B),
                                  MODB[:, part * NMOD:(part + 1) * NMOD].unsqueeze(2).to_broadcast([D, NMOD, B]),
                                  ALU.add).then_inc(S["mod_step"], 1)
            dve.wait_ge(S["mod_step"], 1)
            dve.tensor_scalar(SCL[:, :, :], SCL[:, :, :], 1.0, None, ALU.add).then_inc(S["mod_step"], 1)
            dve.wait_ge(S["mod_step"], 3)
            dve.tensor_tensor(SCL[:, NMOD - 3:NMOD, :], SCL[:, NMOD - 3:NMOD, :],
                              NORMW[:, :].unsqueeze(2).to_broadcast([D, 3, B]), ALU.mult).then_inc(S["mods_ready"], 1)
            dve.wait_ge(S["gatew_in"], 32)
            for k, (lo, hi) in enumerate(((0, 4 * D), (4 * D, NGATE * D))):
                dve.wait_ge(S["g_psum"], k + 1)
                dve.tensor_tensor(G[:, 1, lo:hi], SC[0:B, k, 0:hi - lo], G[:, 0, lo:hi], ALU.add)\
                   .then_inc(S["g_ready"], 1)
            for k in (0, 2, 4, 6):
                dve.tensor_scalar(COLB[:, k:k + 1], COLB[:, k:k + 1], SCALE, None, ALU.mult).then_inc(S["mask_ready"], 1)

            dve.wait_ge(S["ctx_in"], 16)
            with dve.Fori(0, GROUPS) as i:
                for b in range(GB):
                    stats = dve.bn_stats(ST[0:C, b, :], CRAW[0:C, bass.ds(GB * i + b, 1), :])
                stats.then_inc(S["cstats"], 1)
                dve.wait_ge(S["cstats"], i + 1)
                dve.tensor_copy(HOLD[0:C, :], ST[0:C, 0, 0:1])
                for b in range(GB):
                    moments = dve.bn_aggr(MV[0:C, b, :], ST[0:C, b, :])
                moments.then_inc(S["cmoments"], 1)
                dve.wait_ge(S["crstd"], i + 1)
                dve.wait_ge(S["ct_psum"], i)
                for b in range(GB):
                    norm = dve.tensor_scalar(XN[0:C, b, :], CRAW[0:C, bass.ds(GB * i + b, 1), :], MV[0:C, b, 0:1],
                                             RSTD[0:C, b:b + 1], ALU.subtract, ALU.mult)
                norm.then_inc(S["cn_ready"], 1)
            dve.wait_ge(S["ct_psum"], GROUPS)

            def stats(u):
                n = u.n()
                if u.p is not PHASES[0]:
                    dve.wait_ge(S["x_ready"], n - GROUPS + 1)
                for b in range(GB):
                    ins = dve.bn_stats(ST[:, b, :], X[:, bass.ds(u.seq(b), 1), :])
                ins.then_inc(S["ln_stats"], 1)
                wait(dve, "ln_stats", n + 1)
                dve.tensor_copy(HOLD[:, :], ST[:, 0, 0:1])
                for b in range(GB):
                    ins = dve.bn_aggr(MV[:, b, :], ST[:, b, :])
                ins.then_inc(S["ln_moments"], 1)

            def normalise(u):
                n = u.n()
                wait(dve, "rstd_ready", n + 1)
                wait(dve, "xnt_psum", n)
                for b in range(GB):
                    ins = dve.tensor_scalar(XN[:, b, :], X[:, bass.ds(u.seq(b), 1), :], MV[:, b, 0:1],
                                            RSTD[:, b:b + 1], ALU.subtract, ALU.mult)
                ins.then_inc(S["xn_ready"], 1)

            def residual(u):
                n = u.n()
                wait(dve, "y_psum", n + 1)
                wait(dve, "x_ready", n)
                y = PY[:, 0:GB * D].rearrange("p (b d) -> p b d", b=GB)
                if u.p["bias"] is None:
                    dve.tensor_copy(YT[:, :, :], y).then_inc(S["yt_ready"], 1)
                else:
                    row = ROWB[:, u.p["bias"]:u.p["bias"] + 1, :].to_broadcast([N, GB, D])
                    dve.tensor_tensor(YT[:, :, :], y, row, ALU.add).then_inc(S["yt_ready"], 1)

            def projected(u):
                a, end = u.n("att"), width(u)
                wait(dve, "v_psum", a + 1)
                dst = VX if u.kind == SELF else VXC
                k = u.p["att0"] // GROUPS
                dve.tensor_tensor(dst[0:u.T, u.par, :, :], POA[0:u.T, 0:GB * VC].rearrange("p (b c) -> p b c", b=GB),
                                  ROWV[0:u.T, k:k + 1, :].to_broadcast([u.T, GB, VC]), ALU.add)\
                   .then_inc(S["v_ready"], 1)
                if u.p["rope"] is not None:
                    r = u.p["rope"]
                    wait(dve, "qk_psum", a + 1)
                    dve.tensor_tensor(T1[:, 0:end], POB[:, 0:end], RC[:, r, 0:end], ALU.mult)\
                       .then_inc(S["rope_parts"], 1)
                    dve.tensor_tensor(T2[:, 0:end], TR[:, 0:end], RS[:, r, 0:end], ALU.mult)\
                       .then_inc(S["rope_parts"], 1)
                    wait(dve, "rope_parts", 2 * (u.n("rope") + 1))
                    dve.tensor_tensor(QKT[:, 0:end], T1[:, 0:end], T2[:, 0:end], ALU.add)\
                       .then_inc(S["qkt_ready"], 2)
                wait(dve, "part1", a + 1)
                wait(dve, "part3", a)
                dve.tensor_tensor(R1[:, 0:end], QKT[:, 0:end], PT[:, 0, 0:end], ALU.subtract)\
                   .then_inc(S["rest1"], 1)

            def maxima(u, k):
                wait(dve, "s_psum", 4 * u.n("att") + k + 1)
                bank = SC[:, 2 * (k % 2):2 * (k % 2) + 2, 0:HG * u.T].rearrange("p g (h k) -> p g h k", h=HG)
                dve.tensor_reduce(MX[:, 8 * k:8 * k + 8].rearrange("p (g h) -> p g h", g=2), bank, AX.X, ALU.max)\
                   .then_inc(S["mx_ready"], 1)

            def divide(u, b):
                k = 2 * u.n("att") + b
                wait(dve, "tr_psum", k + 1)
                dve.reciprocal(RDEN[:, :], sums).then_inc(S["rden_ready"], 1)
                wait(dve, "rden_ready", k + 1)
                dve.tensor_tensor(OQ[:, b, 0:96].rearrange("p (i t d) -> p i t d", i=3, t=4), own_a,
                                  RDEN[:, 0:12].rearrange("p (i t) -> p i t", i=3).unsqueeze(3)
                                  .to_broadcast([N, 3, 4, HD]), ALU.mult)
                dve.tensor_tensor(OQ[:, b, 96:128].rearrange("p (i t d) -> p i t d", i=2, t=2), own_b,
                                  RDEN[:, 12:16].rearrange("p (i t) -> p i t", i=2).unsqueeze(3)
                                  .to_broadcast([N, 2, 2, HD]), ALU.mult).then_inc(S["oq_ready"], 1)

            def outputs(u, b):
                wait(dve, "o_psum", 2 * u.n("att") + b + 1)
                dve.tensor_copy(OSB[:, b, :], POB[0:N // 2, 0:2 * N]).then_inc(S["ob_ready"], 1)

            def unit(prev, u, nxt, nxt2):
                a = u.n("att")
                if u.attends:
                    maxima(u, 0)
                if prev and prev.attends:
                    divide(prev, 1)
                if u.attends:
                    maxima(u, 1)
                if nxt2:
                    stats(nxt2)
                if nxt and nxt.attends:
                    projected(nxt)
                if prev:
                    residual(prev)
                if u.attends:
                    maxima(u, 2)
                if nxt2:
                    normalise(nxt2)
                if not u.attends:
                    return
                maxima(u, 3)
                wait(dve, "mx_ready", 4 * (a + 1))
                dve.tensor_scalar(MHL[:, 0, 0:GB * H], MX[:, :], -1.0, None, ALU.mult).then_inc(S["neg_hi"], 1)
                wait(dve, "neg_hi", a + 1)
                dve.scalar_tensor_tensor(out=MHL[:, 1, 0:GB * H], in0=MX[:, :], scalar=-1.0, in1=MHL[:, 0, 0:GB * H],
                                         op0=ALU.mult, op1=ALU.subtract).then_inc(S["neg_ready"], 1)
                wait(dve, "m_psum", a + 1)
                dve.tensor_tensor(MBD[:, :, :], PYM.unsqueeze(1).to_broadcast([N, HG, N]),
                                  J4[:, :].unsqueeze(2).to_broadcast([N, HG, N]), ALU.mult).then_inc(S["mbd_ready"], 1)
                outputs(u, 0)
                divide(u, 0)
                outputs(u, 1)

            dve.wait_ge(S["const_in"], 16 * NCONST)
            dve.wait_ge(S["const_set"], 10)
            for k in range(4):
                dve.wait_ge(x_in[k], 16)
            for k in range(2):
                stats(static(k))
                normalise(static(k))
            dve.wait_ge(S["gate_out"], 16)
            projected(static(0))
            run(dve, unit)
            residual(static(GROUPS * len(PHASES) - 1))

        @block.tensor
        def _(pe):
            def mm(o, l, r, start=True, stop=True, **more):
                return pe.matmul(o, l, r, start=start, stop=stop, **more)

            pe.wait_ge(S["cond_ready"], 1)
            for part in range(2):
                pe.wait_ge(S["mods_in"], 16 * (part + 1))
                for k in range(NMOD):
                    at = part * 256 + k * B
                    last = mm(PY[:, at:at + B], MODW[:, k * D:k * D + D], CS[:, 0 if k < 4 else 1, :])
                last.then_inc(S["mod_psum"], 1)
                pe.wait_ge(S["mod_step"], part + 1)
            pe.wait_ge(S["gatew_in"], 32)
            mm(SC[0:B, 0, 0:4 * D], CS[:, 0, :], GATEW[:, 0:4 * D]).then_inc(S["g_psum"], 1)
            mm(SC[0:B, 1, 0:3 * D], CS[:, 1, :], GATEW[:, 4 * D:7 * D]).then_inc(S["g_psum"], 1)
            pe.wait_ge(S["const_in"], 16 * NCONST)
            with pe.Fori(0, GROUPS) as i:
                pe.wait_ge(S["cn_ready"], i + 1)
                pe.wait_ge(S["ct_ready"], i)
                for b in range(GB):
                    last = pe.transpose(TR[:, b * C:b * C + C], XN[0:C, b, :], ID[0:C, 0:C])
                last.then_inc(S["ct_psum"], 1)
            pe.wait_ge(S["ct_ready"], GROUPS)
            pe.wait_ge(S["g_ready"], 2)
            pe.wait_ge(S["const_set"], 10)

            def normed(u):
                wait(pe, "xnt_ready", GB * u.n())
                wait(pe, "xn_ready", u.n() + 1)
                for b in range(GB):
                    last = pe.transpose(TR[:, b * N:b * N + N], XN[:, b, :], ID[:, :])
                last.then_inc(S["xnt_psum"], 1)

            def source(u):
                return XNT[:, u.par, :] if u.kind == SELF else CG[:, u.par, :]

            def project_v(u):
                wait(pe, "xnt_ready", GB * (u.n() + 1))
                if u.kind == CROSS:
                    wait(pe, "cg_ready", u.n("cross") + 1)
                if isinstance(u.i, int) and u.i == 0:
                    layer = u.layer
                    pe.wait_ge(w_in[layer], 16)
                    pe.wait_ge(S["wq_scaled"], 2 * layer + 2 if layer < 2 else 2 * NLAYER + NROPE)
                for b in range(GB):
                    last = mm(POA[0:u.T, b * VC:b * VC + VC], source(u)[:, b * u.T:b * u.T + u.T],
                              wl(u.layer, weights(u)[2], VC))
                last.then_inc(S["v_psum"], 1)

            def project_qk(u):
                wq, wk = [wl(u.layer, k) for k in weights(u)[:2]]
                x, src, end = XNT[:, u.par, :], source(u)[:, 0:GB * u.T], width(u)
                last = mm(POB[:, 0:TOK], wq, x)
                last = mm(POB[:, TOK:end], wk, src)
                if u.p["rope"] is not None:
                    mm(TR[:, 0:TOK], WR[:, u.p["rope"], 0, :], x)
                    last = mm(TR[:, TOK:end], WR[:, u.p["rope"], 1, :], src)
                last.then_inc(S["qk_psum"], 1)

            def keys(u, h, b):
                k = KH[:, u.par, 0:H * GB * u.T].rearrange("p (h t) -> p h t", h=H)
                return k[:, h, b * u.T:b * u.T + u.T]

            def scores(u, k):
                b, a = k // 2, u.n("att")
                if k == 0:
                    wait(pe, "qk_in", 144 * (a + 1))
                    if u.p["mask"] and u.kind == CROSS:
                        wait(pe, "cm_ready", 2 * (u.i + 1))
                if k >= 2:
                    wait(pe, "mx_ready", 4 * a + k - 1)
                masked = u.p["mask"]
                for g in (2 * (k % 2), 2 * (k % 2) + 1):
                    whole = SC[:, g, 0:HG * u.T].rearrange("p (h k) -> p h k", h=HG)
                    if masked and u.kind == SELF:
                        mm(whole, IDB[:, :], SM[:, :].unsqueeze(1).to_broadcast([N, HG, N]), stop=False,
                           skip_group_check=True)
                    elif masked:
                        mm(whole, ONE[:, :], CMG[:, u.par, b:b + 1, :].to_broadcast([N, HG, C]), stop=False,
                           skip_group_check=True)
                    for j in range(HG):
                        last = mm(whole[:, j, :], QH[:, u.par, HG * g + j, b * N:b * N + N], keys(u, HG * g + j, b),
                                  start=not masked, skip_group_check=masked)
                last.then_inc(S["s_psum"], 1)

            def shifted(u, k):
                b, pr = divmod(k, 2)
                a = u.n("att")
                if k >= 2:
                    wait(pe, "p_ready", 4 * a + k - 1)
                masked = u.p["mask"] and u.kind == SELF
                for g in (2 * pr, 2 * pr + 1):
                    dst = SC[0:u.T, g, :].rearrange("p (h q) -> p h q", h=HG)
                    if masked:
                        mm(dst, SM[:, :], IDB[:, :].unsqueeze(1).to_broadcast([N, HG, N]), stop=False,
                           skip_group_check=True)
                    else:
                        mm(dst, SEL[:, NHG * b + g, 0:u.T], MBD[:, :, :], stop=False, skip_group_check=True)
                    for j in range(HG):
                        last = mm(dst[:, j, :], keys(u, HG * g + j, b), QH[:, u.par, HG * g + j, b * N:b * N + N],
                                  start=False, stop=not masked, skip_group_check=True)
                    if masked:
                        last = mm(dst, SEL[:, NHG * b + g, 0:u.T], MBD[:, :, :], start=False, skip_group_check=True)
                last.then_inc(S["st_psum"], 1)

            def values(u, b):
                wait(pe, "p_ready", 4 * u.n("att") + 2 * b + 2)
                v = (VX if u.kind == SELF else VXC)[:, u.par, b, :]
                for t, heads in enumerate(TILE_HEADS):
                    bank, row = (POA, t) if t < 4 else (POB, t - 4)
                    n = len(heads) * N
                    last = mm(bank[VW * row:VW * row + VW, 0:n], v[:, VW * t:VW * t + VW],
                              PR[:, b, heads[0] * N:heads[0] * N + n])
                last.then_inc(S["o_psum"], 1)

            def to_rows(u, b):
                k = 2 * u.n("att") + b
                wait(pe, "oa_ready", k + 1)
                wait(pe, "ob_ready", k + 1)
                for i in range(3):
                    pe.transpose(TR[:, i * N:i * N + N], OSA[:, b, i * N:i * N + N], ID[:, :])
                for i in range(2):
                    at = 3 * N + i * N // 2
                    last = pe.transpose(TR[:, at:at + N // 2], OSB[:, b, i * N:i * N + N], ID[0:N // 2, 0:N // 2])
                last.then_inc(S["tr_psum"], 1)

            def to_features(u, b):
                wait(pe, "oq_ready", 2 * u.n("att") + b + 1)
                pe.transpose(PYOT, OQ[:, b, :], ID[:, :]).then_inc(S["ot_psum"], 1)

            def project_out(u, b):
                wait(pe, "ot_ready", 2 * u.n("att") + b + 1)
                last = mm(PY[:, b * D:b * D + D], OT[:, b, :], wl(u.layer, weights(u)[3]))
                if b == GB - 1:
                    last.then_inc(S["y_psum"], 1)

            def unit(prev, u, nxt, nxt2):
                a, n = u.n("att"), u.n()
                late = prev and prev.attends
                ahead = nxt and nxt.attends
                if u.attends:
                    scores(u, 0)
                else:
                    wait(pe, "xnt_ready", GB * (n + 1))
                    for c in range(2):
                        mm(SC[:, c, 0:TOK], wl(u.layer, W1 + c * D), XNT[:, u.par, :]).then_inc(S["h_psum"], 1)
                if late:
                    to_rows(prev, 1)
                if u.attends:
                    scores(u, 1)
                else:
                    for c in range(2, NC):
                        mm(SC[:, c, 0:TOK], wl(u.layer, W1 + c * D), XNT[:, u.par, :]).then_inc(S["h_psum"], 1)
                if ahead:
                    project_v(nxt)
                if late:
                    to_features(prev, 1)
                if ahead:
                    project_qk(nxt)
                if late:
                    project_out(prev, 1)
                if u.attends:
                    scores(u, 2)
                    scores(u, 3)
                if nxt2:
                    if ahead:
                        wait(pe, "qkt_ready", 2 * (nxt.n("att") + 1))
                    normed(nxt2)
                if ahead:
                    wait(pe, "v_ready", nxt.n("att") + 1)
                wait(pe, "yt_ready", n)
                if not u.attends:
                    wait(pe, "h_ready", NC * (u.n("mlp") + 1))
                    for b in range(GB):
                        for c in range(NC):
                            last = mm(PY[:, b * D:b * D + D], HT[:, c, b * N:b * N + N], wl(u.layer, W2 + c * D),
                                      start=c == 0, stop=c == NC - 1)
                    last.then_inc(S["y_psum"], 1)
                    return
                wait(pe, "neg_ready", a + 1)
                pe.transpose(PYM, MHL[:, :, :].rearrange("p a c -> p (a c)"), IDB[:, :]).then_inc(S["m_psum"], 1)
                wait(pe, "mbd_ready", a + 1)
                shifted(u, 0)
                shifted(u, 1)
                shifted(u, 2)
                values(u, 0)
                shifted(u, 3)
                if nxt2:
                    wait(pe, "xnt_ready", GB * (nxt2.n() + 1))
                to_rows(u, 0)
                values(u, 1)
                to_features(u, 0)
                project_out(u, 0)

            normed(static(0))
            normed(static(1))
            project_v(static(0))
            project_qk(static(0))
            pe.wait_ge(S["xnt_ready"], 2 * GB)
            pe.wait_ge(S["v_ready"], 1)
            pe.wait_ge(S["qkt_ready"], 2)
            run(pe, unit)


def kernel(**inputs):
    import ml_dtypes
    import concourse.bacc as bacc
    from concourse.bass_utils import run_bass_kernel_spmd

    t = {k: np.asarray(v) for k, v in inputs.items()}
    L = [{k[9:]: v for k, v in t.items() if k.startswith(f"L{n}_xcond_")} for n in range(4)]
    a, b, c, d = L

    def cut(m, n):
        return m[..., n * D:(n + 1) * D]

    by_width = np.arange(D).reshape(H, HD).T.reshape(-1)
    swap = np.arange(D).reshape(H, 2, HD // 2)[:, ::-1].reshape(-1)[by_width]
    outs = np.concatenate([np.arange(h * HD, h * HD + HD) for h in OUT_HEADS])

    def tiles(m, one=0.0):
        r = np.zeros(m.shape[:-1] + (VT, VW), m.dtype)
        for k, heads in enumerate(TILE_HEADS):
            r[..., k, 0:HD * len(heads)] = m[..., heads[0] * HD:(heads[-1] + 1) * HD]
        r[..., ONE_AT] = one
        return r.reshape(m.shape[:-1] + (VC,))

    def blocks(wt):
        return np.concatenate([wt[k * D:k * D + D] for k in range(NC)], axis=1)

    def layer(q, k, v, o, cq, ck, cv, co, w1, w2):
        return np.concatenate([q[:, by_width], k[:, by_width], tiles(v), o[outs], cq[:, by_width], ck[:, by_width],
                               tiles(cv), co[outs], w1, blocks(w2)], axis=1)

    qkv2 = c["qkv_w"].T
    w = np.stack([
        layer(*[cut(a["W_qkv"], n) for n in range(3)], a["W_proj"], a["W_qc"], cut(a["W_kvc"], 0), cut(a["W_kvc"], 1),
              a["W_cproj"], a["W_mlp1"], a["W_mlp2"]),
        layer(*[cut(b["qkv_w"], n) for n in range(3)], b["sa_proj_w"], b["q_w"], cut(b["kv_w"], 0), cut(b["kv_w"], 1),
              b["ca_proj_w"], b["fc1_w"], b["fc2_w"]),
        layer(*[cut(qkv2, n) for n in range(3)], c["sa_out_w"].T, c["q_w"].T, c["k_w"].T, c["v_w"].T,
              c["ca_out_w"].T, c["ffn_w1"].T, c["ffn_w2"].T),
        layer(*[cut(d["qkv_W"], n) for n in range(3)], d["attn_out_W"], d["cq_W"], d["ck_W"], d["cv_W"],
              d["co_W"], d["mlp_W1"], d["mlp_W2"]),
    ])
    wrot = np.stack([m[:, swap] for m in (cut(qkv2, 0), cut(qkv2, 1), c["q_w"].T, c["k_w"].T, cut(d["qkv_W"], 0),
                                          cut(d["qkv_W"], 1))], axis=1).reshape(D, NROPE, 2, D)

    lns = [(c[f"ln{k}_w"].T, c[f"ln{k}_b"]) for k in (1, 2, 3)]
    scale = [(a["W_mod"], a["b_mod"], 1), (a["W_mod"], a["b_mod"], 4), (b["adaln_w"], b["adaln_b"], 1),
             (b["adaln_w"], b["adaln_b"], 4)] + [(x, y, 0) for x, y in lns] + \
            [(d["adaLN_W"], d["adaLN_b"], k) for k in (1, 4, 7)]
    shift = [(a["W_mod"], a["b_mod"], 0), (a["W_mod"], a["b_mod"], 3), (b["adaln_w"], b["adaln_b"], 0),
             (b["adaln_w"], b["adaln_b"], 3)] + [(x, y, 1) for x, y in lns] + \
            [(d["adaLN_W"], d["adaLN_b"], k) for k in (0, 3, 6)]
    gate = [(a["W_mod"], a["b_mod"], 2), (a["W_mod"], a["b_mod"], 5), (b["adaln_w"], b["adaln_b"], 2),
            (b["adaln_w"], b["adaln_b"], 5)] + [(d["adaLN_W"], d["adaLN_b"], k) for k in (2, 5, 8)]
    modw = np.concatenate([cut(x, n) for x, _, n in scale + shift], axis=1)
    modb = np.stack([cut(y, n) for _, y, n in scale + shift], axis=1)
    gatew = np.concatenate([cut(x, n) for x, _, n in gate], axis=1)
    gateb = np.concatenate([cut(y, n) for _, y, n in gate])
    colb = np.stack([m[by_width] for m in (cut(a["b_qkv"], 0), cut(a["b_qkv"], 1), a["b_qc"], cut(a["b_kvc"], 0),
                                           cut(b["qkv_b"], 0), cut(b["qkv_b"], 1), b["q_b"], cut(b["kv_b"], 0))],
                    axis=1)
    rowb = np.stack([a["b_proj"], a["b_cproj"], a["b_mlp2"], b["sa_proj_b"], b["ca_proj_b"], b["fc2_b"],
                     c["ffn_b2"], d["mlp_b2"]])
    rowv = np.stack([tiles(m, 1.0) for m in (cut(a["b_qkv"], 2), cut(a["b_kvc"], 1), cut(b["qkv_b"], 2),
                                             cut(b["kv_b"], 1))] + [tiles(np.zeros(D, np.float32), 1.0)] * 4)
    mlpb = np.stack([x.reshape(NC, D).T for x in (a["b_mlp1"], b["fc1_b"], c["ffn_b1"], d["mlp_b1"])], axis=1)

    row = np.arange(N)
    jmask4 = (row[:, None] % HG == np.arange(HG)).astype(np.float32)
    sel = np.repeat((row[:, None] % (N // 2) // HG == np.arange(GB * NHG))[:, :, None], N, axis=2)\
        .astype(ml_dtypes.bfloat16)
    half = HD // 2
    width = row // H
    freq = (1.0 / 10000.0 ** (np.arange(half, dtype=np.float32) / half)).astype(np.float32)[width % half]
    tok = np.arange(N)
    pos = np.zeros((NROPE, 2 * TOK), np.float32)
    pos[0] = np.tile(tok, 2 * GB)
    pos[1, :TOK] = np.tile(tok, GB)
    pos[1, TOK:TOK + GB * C] = np.tile(np.arange(C), GB)
    pos[2] = np.tile(tok % (N // 2), 2 * GB)
    ang = freq[:, None, None] * pos[None]
    sign = np.where(width < half, -1.0, 1.0).astype(np.float32)[:, None, None]
    arrays = dict(
        x=t["x"], cond_t=t["cond_1024"].T, ctx_tok=t["ctx_1024"], ctx_t=t["ctx_1024"].reshape(B * C, D).T,
        w=w, wrot=wrot, modw=modw, modb=modb, gatew=gatew, gateb=gateb,
        normw=np.stack([d["norm1_w"], d["normc_w"], d["norm2_w"]], axis=1), colb=colb, rowb=rowb, rowv=rowv,
        mlpb=mlpb, smask=t["mask_SxS_bk0"], cmask=t["mask_BxS2_bf1"].reshape(1, B * C),
        cmask_t=t["mask_BxS2_bf1"].T,
        ident=np.eye(N, dtype=np.float32), identb=np.eye(N, dtype=np.float32).astype(ml_dtypes.bfloat16),
        jmask4=jmask4, sel=sel,
        ropec=np.cos(ang).astype(np.float32), ropes=(np.sin(ang) * sign).astype(np.float32))
    arrays = {"in_" + k: np.ascontiguousarray(v) for k, v in arrays.items()}
    nc = bacc.Bacc("TRN2", target_bir_lowering=False, num_devices=1)
    args = {k[3:]: nc.dram_tensor(k, v.shape, mybir.dt.from_np(v.dtype), kind="ExternalInput").ap()
            for k, v in arrays.items()}
    out = nc.dram_tensor("out", (B, N, D), F32, kind="ExternalOutput").ap()
    build(nc, out=out, **args)
    r = run_bass_kernel_spmd(nc, [arrays], core_ids=[0])
    return r.results[0]["out"]
```

```python
from contextlib import ExitStack

import numpy as np

import concourse.bass as bass
from concourse import mybir

ALU = mybir.AluOpType
ACT = mybir.ActivationFunctionType
AX = mybir.AxisListType
F32 = mybir.dt.float32
BF16 = mybir.dt.bfloat16
U8 = mybir.dt.uint8

B, N, D = 16, 128, 128
H, HD = 16, 8
C = 77
FF = 512
NC = FF // D
GB = 2
GROUPS = B // GB
TOK = GB * N
HG = 4
NHG = H // HG
PARTS = 3
STACK = (3, 2, 1)
LOADS = 32 * len(STACK)
VT, VW = 6, 32
ONE_AT = 24
TILE_HEADS = [[0, 1, 2], [3, 4, 5], [6, 7, 8], [9, 10, 11], [12, 13], [14, 15]]
OUT_HEADS = [TILE_HEADS[t][k] for k in range(3) for t in range(4)] + [12, 14, 13, 15]
SCALE = float(HD) ** -0.5
BIG = 3.3895313892515355e38

SELF, CROSS, MLP = range(3)


def phase(kind, layer, **more):
    p = dict(kind=kind, layer=layer, mod=None, gate=None, bias=None, qk=None, rope=None, mask=False, eps=0,
             gelu=None)
    p.update(more)
    return p


PHASES = [
    phase(SELF, 0, mod=0, gate=0, bias=0, qk=0),
    phase(CROSS, 0, bias=1, qk=2),
    phase(MLP, 0, mod=1, gate=1, bias=2, gelu="tanh"),
    phase(SELF, 1, mod=2, gate=2, bias=3, qk=4),
    phase(CROSS, 1, bias=4, qk=6),
    phase(MLP, 1, mod=3, gate=3, bias=5, gelu="tanh"),
    phase(SELF, 2, mod=4, rope=0, eps=1),
    phase(CROSS, 2, mod=5, rope=1, eps=1),
    phase(MLP, 2, mod=6, bias=6, eps=1, gelu="erf"),
    phase(SELF, 3, mod=7, gate=4, rope=2, mask=True, eps=1),
    phase(CROSS, 3, mod=8, gate=5, mask=True, eps=1),
    phase(MLP, 3, mod=9, gate=6, bias=7, eps=1, gelu="tanh"),
]
NMOD, NGATE, NBIAS, NLAYER, NROPE = 10, 7, 8, 4, 3
NEXT = dict(unit=0, att=0, mlp=0, rope=0, gated=0, cross=0)
for p_ in PHASES:
    p_.update({k + "0": v for k, v in NEXT.items()})
    NEXT["unit"] += GROUPS
    NEXT["att"] += GROUPS * (p_["kind"] != MLP)
    NEXT["mlp"] += GROUPS * (p_["kind"] == MLP)
    NEXT["rope"] += GROUPS * (p_["rope"] is not None)
    NEXT["gated"] += GROUPS * (p_["gate"] is not None)
    NEXT["cross"] += GROUPS * (p_["kind"] == CROSS)


class Unit:

    def __init__(self, p, i, parity):
        self.p, self.i, self.par = p, i, parity
        self.kind, self.layer = p["kind"], p["layer"]
        self.T = N if self.kind == SELF else C
        self.attends = self.kind != MLP

    def n(self, sort="unit"):
        return self.p[sort + "0"] + self.i

    def seq(self, b=0):
        return GB * self.i + b


def static(n):
    if 0 <= n < GROUPS * len(PHASES):
        return Unit(PHASES[n // GROUPS], n % GROUPS, n % 2)
    return None


class Rows:

    def __init__(self, n, i, parity):
        self.number, self.i, self.par = n, i, parity

    def n(self):
        return self.number

    def seq(self, b=0):
        return GB * self.i + b


def alone(unit, n):
    third = n + 3
    rows = Rows(third, third % GROUPS, third % 2) if third < GROUPS * len(PHASES) else None
    unit(*[static(m) for m in (n - 1, n, n + 1, n + 2)], rows)


def run(eng, unit):
    for k, p in enumerate(PHASES):
        first = GROUPS * k
        if p is PHASES[-1]:
            for n in range(first, first + GROUPS + 1):
                alone(unit, n)
            return
        alone(unit, first)
        alone(unit, first + 1)
        with eng.Fori(1, GROUPS // 2 - 1) as pair:
            for odd in range(2):
                third = pair * 2 + (odd + 3)
                unit(*[Unit(p, pair * 2 + (odd + m), (odd + m) % 2) for m in (-1, 0, 1, 2)],
                     Rows(third + first, third % GROUPS if odd else third, (odd + 3) % 2))
        alone(unit, first + GROUPS - 2)
        alone(unit, first + GROUPS - 1)


VC = VT * VW
WQ, WK, WV, WO, CQ, CK, CV, CO, W1, W2, WEND = np.cumsum([0, D, D, VC, D, D, D, VC, D, FF, FF]).tolist()

def build(nc, x, cond_t, ctx_tok, ctx_t, w, wrot, modw, modb, gatew, gateb, normw, colb, rowb, rowv, mlpb,
          smask, cmask, cmask_t, ident, identb, jmask4, sel, ropec, ropes, out):
    with ExitStack() as ctx:
        def sb(name, shape, dt=F32):
            return ctx.enter_context(nc.sbuf_tensor(name, shape, dt))

        X = sb("X", [N, B, D])
        W = sb("W", [D, NLAYER, WEND])
        WR = sb("WR", [D, NROPE, 2, D])
        SCL = sb("SCL", [D, NMOD, B])
        SHF = sb("SHF", [D, NMOD, B])
        CTXT = sb("CTXT", [D, B * C])
        CTXN = sb("CTXN", [D, B * C])
        COLB = sb("COLB", [D, 8])
        ROWB = sb("ROWB", [N, NBIAS, D])
        ROWV = sb("ROWV", [N, 8, VC])
        MLPB = sb("MLPB", [D, NLAYER, NC])
        ID = sb("ID", [N, N])
        IDB = sb("IDB", [N, N], BF16)
        J4 = sb("J4", [N, HG])
        SEL = sb("SEL", [N, GB * NHG, N], BF16)
        RC = sb("RC", [D, NROPE, 2 * TOK])
        RS = sb("RS", [D, NROPE, 2 * TOK])
        SM = sb("SM", [N, N], BF16)
        CM = sb("CM", [N, B, C], BF16)
        CMT = sb("CMT", [C, B])
        ONE = sb("ONE", [N, N], BF16)
        NHALF = sb("NHALF", [N, B])
        EPS = sb("EPS", [N, len(PHASES) * GROUPS * GB])
        LSC = sb("LSC", [D, len(PHASES), B])
        LSH = sb("LSH", [D, len(PHASES), B])
        XN = sb("XN", [N, GB, D])
        ST = sb("STAT", [N, GB, 6])
        HOLD = sb("HOLD", [N, 1])
        HELD = sb("HELD", [N, 1])
        MV = sb("MV", [N, GB, 2])
        VE = sb("VE", [N, GB])
        RSTD = sb("RSTD", [N, GB])
        XNT = sb("XNT", [D, 2, TOK])
        GATE = sb("GATE", [N, 2, GB, D])
        CG = sb("CG", [D, 2, GB * C])
        CMG = sb("CMG", [N, 2, GB, C], BF16)
        CMTG = sb("CMTG", [C, 2, GB])
        WORK = sb("WORK", [D, 4, 2 * TOK])
        QKT, T1, T2, R1 = [WORK[:, k, :] for k in range(4)]
        PT = sb("PT", [D, PARTS, 2 * TOK], BF16)
        QH = sb("QH", [N, 2, H, TOK], BF16)
        KH = sb("KH", [N, 2, H * TOK], BF16)
        VX = sb("VX", [N, 2, GB, VC])
        VXC = sb("VXC", [N, 2, GB, VC])
        MX = sb("MX", [N, GB * H])
        MHL = sb("MHL", [N, 2, N // 2], BF16)
        MBD = sb("MBD", [N, 2, HG, N], BF16)
        PR = sb("PR", [N, GB, H * N])
        HT = sb("HT", [D, 2, NC, TOK])
        OSA = sb("OSA", [N, GB, 3 * N])
        OSB = sb("OSB", [N // 2, GB, 2 * N])
        RDEN = sb("RDEN", [N, H])
        OQ = sb("OQ", [N, GB, D])
        OT = sb("OT", [D, GB, N])
        YT = sb("YT", [N, 2, GB, D])
        CRAW = PR[:, 0, :].rearrange("p (b d) -> p b d", b=B)
        GATEW = HT[:, :, :, :].rearrange("p u c t -> p (u c t)")[:, 0:NGATE * D]
        G = WORK[0:B, :, :].rearrange("p a t -> p (a t)")[:, 0:2 * NGATE * D].rearrange("p (a c) -> p a c", a=2)
        MODW = sb("MODW", [D, 2, NMOD * D])
        CST = sb("CST", [C, B, 6])
        CMV = sb("CMV", [C, B, 2])
        CVE = sb("CVE", [C, 2, B])
        CS = sb("CS", [D, 2, B])
        CT = sb("CT", [D, 3, B])
        MODB = sb("MODB", [D, 2 * NMOD])
        NORMW = sb("NORMW", [D, 3])
        MU8 = sb("MU8", [N, N + B], U8)
        CM8 = sb("CM8", [1, B * C], U8)
        gate_dram = nc.dram_tensor("gate_rows", (B, NGATE * D), F32, kind="Internal").ap()
        q_dram = nc.dram_tensor("q_parts", (2, PARTS, D, TOK), BF16, kind="Internal").ap()
        ks_dram = nc.dram_tensor("k_parts", (2, PARTS, D, TOK), BF16, kind="Internal").ap()
        kc_dram = nc.dram_tensor("k_context_parts", (2, PARTS, D, GB * C), BF16, kind="Internal").ap()

        SC = ctx.enter_context(nc.psum_tensor("SC", [N, 4, 512], F32))
        POA = ctx.enter_context(nc.psum_tensor("POA", [N, 512], F32))
        POB = ctx.enter_context(nc.psum_tensor("POB", [N, 512], F32))
        TP = ctx.enter_context(nc.psum_tensor("TP", [N, 2, 512], F32))
        TR, PY = TP[:, 0, :], TP[:, 1, :]
        PYOT = PY[:, 2 * D:3 * D]
        PYM = PY[:, 3 * D:3 * D + N // 2].bitcast(BF16)
        flat = TP[:, :, :].rearrange("p a c -> p (a c)")
        own_a = flat[:, 0:3 * (N + HD)].rearrange("p (i s) -> p i s", s=N + HD)[:, :, 0:N]\
            .rearrange("p i (t c) -> p i t c", c=VW)[:, :, :, 0:HD]
        own_b = flat[:, 3 * N:3 * N + 2 * (N // 2 + HD)].rearrange("p (i s) -> p i s", s=N // 2 + HD)[:, :, 0:N // 2]\
            .rearrange("p i (t c) -> p i t c", c=VW)[:, :, :, 0:HD]
        sums = TR.rearrange("p (n c) -> p n c", c=VW)[:, :, ONE_AT]

        names = ("cond_in mods_in gatew_in small_in modb_in rows_in ctx_in ctxt_in const_in wrot_in gate_out gate_in out_done "
                 "silu_exp silu_step cond_ready mod_psum mod_step mods_ready lset kh_zero ls_ready g_psum g_ready mask_ready const_set "
                 "wq_scaled cstats cmoments cvar crstd cn_ready ct_psum ct_ready "
                 "ln_stats ln_moments var_eps rstd_ready xn_ready xnt_psum xnt_ready cg_ready cm_ready "
                 "qk_psum v_psum rope_parts rotated part1 rest1 part2 part3 parts_out qk_in v_ready "
                 "s_psum mx_ready neg_hi neg_ready m_psum mbd_ready st_psum p_ready o_psum oa_ready ob_ready "
                 "tr_psum rden_ready oq_ready ot_psum ot_ready y_psum yt_ready gated x_ready h_psum h_ready").split()
        S = {k: ctx.enter_context(nc.semaphore("s_" + k)) for k in names}
        x_in = [ctx.enter_context(nc.semaphore(f"s_x_in{i}")) for i in range(4)]
        w_in = [ctx.enter_context(nc.semaphore(f"s_w_in{i}")) for i in range(NLAYER)]
        block = ctx.enter_context(nc.Block())
        NCONST, NSMALL = 6, 5
        per_bank = 512 // C
        CBANKS = [(lo, min(lo + per_bank, B)) for lo in range(0, B, per_bank)]

        def wait(eng, name, value):
            if not isinstance(value, int) or value > 0:
                eng.wait_ge(S[name], value)

        def wl(layer, at, width=D):
            return W[:, layer, at:at + width]

        def weights(u):
            return (WQ, WK, WV, WO) if u.kind == SELF else (CQ, CK, CV, CO)

        def width(u):
            return TOK + GB * u.T

        def k_dram(u):
            return ks_dram if u.kind == SELF else kc_dram

        @block.sync
        def _(sp):
            sp.dma_start(CS[:, 1, :], cond_t).then_inc(S["cond_in"], 16)
            for k in range(4):
                sp.dma_start(X[:, 4 * k:4 * k + 4, :],
                             x[4 * k:4 * k + 4].rearrange("b t d -> t b d")).then_inc(x_in[k], 16)
                if k == 0:
                    sp.dma_start(W[:, 0, :], w[0]).then_inc(w_in[0], 16)
                    sp.dma_start(CRAW[0:C, :, :], ctx_tok.rearrange("b c d -> c b d")).then_inc(S["ctx_in"], 16)
            sp.wait_ge(S["g_ready"], 2)
            sp.dma_start(gate_dram, G[:, 1, :]).then_inc(S["gate_out"], 16)
            sp.wait_ge(S["gate_out"], 16)
            sp.wait_ge(S["const_set"], 7)
            sp.wait_ge(S["kh_zero"], 1)

            def ahead(*values):
                return [v if isinstance(v, int) else sp.to_reg(v) for v in values]

            def stack(u):
                a = u.n("att")
                loaded, split, left, used = ahead(LOADS * a, a + 1, 32 * (a + 1), 4 * (a - 1))
                wait(sp, "qk_in", loaded)
                wait(sp, "part3", split)
                sp.dma_start(q_dram[u.par].rearrange("x r t -> r x t"), PT[:, :, 0:TOK]).then_inc(S["parts_out"], 16)
                sp.dma_start(k_dram(u)[u.par].rearrange("x r t -> r x t"), PT[:, :, TOK:width(u)])\
                  .then_inc(S["parts_out"], 16)
                wait(sp, "parts_out", left)
                wait(sp, "st_psum", used)
                row = 0
                for part, n in enumerate(STACK):
                    sp.dma_start(QH[row:row + HD * n, u.par, :, :].rearrange("r h t -> r (h t)"),
                                 q_dram[u.par, 0:n].rearrange("x (d h) t -> (x d) (h t)", d=HD)).then_inc(S["qk_in"], 16)
                    sp.dma_start(KH[row:row + HD * n, u.par, 0:H * GB * u.T],
                                 k_dram(u)[u.par, part].rearrange("(d h) t -> d (h t)", d=HD)
                                 .unsqueeze(0).to_broadcast([n, HD, H * GB * u.T])).then_inc(S["qk_in"], 16)
                    row += HD * n

            def gates(u):
                if u.p["gate"] is not None:
                    used, last = ahead(u.n() - 1 + GROUPS, 16 * u.n("gated"))
                    wait(sp, "x_ready", used)
                    wait(sp, "gate_in", last)
                    at = u.p["gate"] * D
                    sp.dma_start(GATE[:, u.par, :, :],
                                 gate_dram[bass.ds(u.seq(), GB), at:at + D].partition_broadcast(N))\
                      .then_inc(S["gate_in"], 16)

            def unit(prev, u, nxt, nxt2, rows):
                if nxt2 and nxt2.attends:
                    stack(nxt2)
                if nxt:
                    gates(nxt)
                if prev and prev.p is PHASES[-1]:
                    wait(sp, "x_ready", *ahead(prev.n() + 1 + GROUPS))
                    sp.dma_start(out[bass.ds(prev.seq(), GB)].rearrange("b t d -> t b d"),
                                 X[:, bass.ds(prev.seq(), GB), :]).then_inc(S["out_done"], 16)

            alone(unit, -3)
            alone(unit, -2)
            for layer in range(1, NLAYER):
                sp.dma_start(W[:, layer, :], w[layer]).then_inc(w_in[layer], 16)
            sp.dma_start(WR[:, :, :, :], wrot).then_inc(S["wrot_in"], 16)
            sp.dma_start(CTXT[:, :], ctx_t).then_inc(S["ctxt_in"], 16)
            alone(unit, -1)
            run(sp, unit)
            sp.wait_ge(S["out_done"], 16 * GROUPS)

        @block.scalar
        def _(act):
            act.dma_start(MODB[:, :], modb).then_inc(S["modb_in"], 16)
            act.dma_start(NORMW[:, :], normw).then_inc(S["modb_in"], 16)
            for part in range(2):
                act.dma_start(MODW[:, part, :], modw[:, part * NMOD * D:(part + 1) * NMOD * D])\
                   .then_inc(S["mods_in"], 16)
            act.wait_ge(S["cond_in"], 16)
            act.activation(CT[:, 0, :], CS[:, 1, :], ACT.Exp, scale=-1.0).then_inc(S["silu_exp"], 1)
            act.dma_start(ID[:, :], ident).then_inc(S["const_in"], 16)
            act.dma_start(GATEW, gatew).then_inc(S["gatew_in"], 16)
            act.dma_start(G[:, 0, :], gateb.partition_broadcast(B)).then_inc(S["gatew_in"], 16)
            act.dma_start(COLB[:, :], colb).then_inc(S["small_in"], 16)
            act.dma_start(MLPB[:, :, :], mlpb).then_inc(S["small_in"], 16)
            act.dma_start(MU8[:, 0:N], smask).then_inc(S["small_in"], 16)
            act.dma_start(MU8[0:C, N:N + B], cmask_t).then_inc(S["small_in"], 16)
            act.dma_start(CM8[:, :], cmask).then_inc(S["small_in"], 16)
            for dst, src in ((IDB[:, :], identb), (J4[:, :], jmask4), (SEL[:, :, :], sel),
                             (RC[:, :, :], ropec), (RS[:, :, :], ropes)):
                act.dma_start(dst, src).then_inc(S["const_in"], 16)
            act.dma_start(ROWB[:, :, :], rowb.partition_broadcast(N)).then_inc(S["rows_in"], 16)
            act.dma_start(ROWV[:, :, :], rowv.partition_broadcast(N)).then_inc(S["rows_in"], 16)
            scales, shifts = [t[:, :, :].rearrange("p k b -> p (k b)") for t in (LSC, LSH)]

            def normed(u):
                wait(act, "xnt_psum", u.n() + 1)
                for b in range(GB):
                    row = bass.ds(GB * u.n() + b, 1)
                    act.activation(XNT[:, u.par, b * N:b * N + N], TR[:, b * N:b * N + N], ACT.Identity,
                                   bias=shifts[:, row], scale=scales[:, row]).then_inc(S["xnt_ready"], 1)

            def first_part(u):
                a, end = u.n("att"), width(u)
                wait(act, "parts_out", 32 * a)
                if u.p["rope"] is not None:
                    wait(act, "rotated", u.n("rope") + 1)
                    act.activation(PT[:, 0, 0:end], QKT[:, 0:end], ACT.Copy).then_inc(S["part1"], 1)
                    return
                wait(act, "qk_psum", a + 1)
                if u.p["qk"] is None:
                    act.activation(PT[:, 0, 0:end], POB[:, 0:end], ACT.Copy).then_inc(S["part1"], 1)
                    return
                for k, (lo, hi) in enumerate(((0, TOK), (TOK, end))):
                    c = u.p["qk"] + k
                    last = act.activation(PT[:, 0, lo:hi], POB[:, lo:hi], ACT.Identity, bias=COLB[:, c:c + 1])
                last.then_inc(S["part1"], 1)

            def second_part(u):
                a, end = u.n("att"), width(u)
                wait(act, "rest1", a + 1)
                act.activation(PT[:, 1, 0:end], R1[:, 0:end], ACT.Copy).then_inc(S["part2"], 1)

            def transposed(u, b):
                wait(act, "ot_psum", 2 * u.n("att") + b + 1)
                act.activation(OT[:, b, :], PYOT, ACT.Copy).then_inc(S["ot_ready"], 1)

            def probabilities(u, k):
                b, pr = divmod(k, 2)
                more = {}
                if u.p["mask"] and u.kind == CROSS:
                    more = dict(bias=CMTG[:, u.par, b:b + 1])
                wait(act, "st_psum", 4 * u.n("att") + k + 1)
                act.activation(PR[0:u.T, b, pr * 1024:pr * 1024 + 1024], SC[0:u.T, 2:4, :],
                               ACT.Exp, **more).then_inc(S["p_ready"], 1)

            def outputs(u, b):
                wait(act, "o_psum", 2 * u.n("att") + b + 1)
                act.activation(OSA[:, b, :], POA[:, 0:3 * N], ACT.Copy).then_inc(S["oa_ready"], 1)

            def hidden(u):
                f = ACT.Gelu if u.p["gelu"] == "erf" else ACT.Gelu_apprx_tanh
                for c in range(NC):
                    wait(act, "h_psum", NC * u.n("mlp") + c + 1)
                    act.activation(HT[:, u.par, c, :], SC[:, c, 0:TOK], f,
                                   bias=MLPB[:, u.layer, c:c + 1]).then_inc(S["h_ready"], 1)

            def unit(prev, u, nxt, nxt2, rows):
                late = prev and prev.attends
                now = u and u.attends
                soon = nxt and nxt.attends
                lone = nxt and not soon and now
                ahead = nxt2 and nxt2.attends
                if now:
                    if u.p["mask"] and u.kind == CROSS:
                        wait(act, "cm_ready", 2 * (u.i + 1))
                    probabilities(u, 0)
                if ahead:
                    first_part(nxt2)
                turned = ahead and nxt2.p["rope"] is not None
                if late and not turned:
                    transposed(prev, 0)
                if now:
                    probabilities(u, 1)
                if ahead:
                    second_part(nxt2)
                if late and turned:
                    transposed(prev, 0)
                if now:
                    probabilities(u, 2)
                if late:
                    transposed(prev, 1)
                if now:
                    outputs(u, 0)
                    probabilities(u, 3)
                if rows and not lone:
                    if nxt and not soon:
                        hidden(nxt)
                    normed(rows)
                if now:
                    outputs(u, 1)
                if lone or not rows:
                    if nxt and not soon:
                        hidden(nxt)
                    if rows:
                        normed(rows)

            act.wait_ge(S["ls_ready"], 6)
            alone(unit, -3)
            act.wait_ge(S["const_in"], 16 * NCONST)
            act.wait_ge(S["mask_ready"], 7)
            act.wait_ge(S["gate_out"], 16)
            alone(unit, -2)
            for k, (lo, hi) in enumerate(CBANKS):
                act.wait_ge(S["ct_psum"], k + 1)
                act.activation(CTXN[:, C * lo:C * hi], SC[:, k, 0:C * (hi - lo)], ACT.Copy).then_inc(S["ct_ready"], 1)
            alone(unit, -1)
            run(act, unit)

        @block.gpsimd
        def _(pool):
            def hold():
                return pool.tensor_tensor(HELD[:, :], NHALF[:, 0:1], NHALF[:, 0:1], ALU.mult)

            pool.memset(NHALF[:, :], -0.5).then_inc(S["const_set"], 1)
            per = GROUPS * GB
            fine = [p["eps"] for p in PHASES].index(1) * per
            pool.memset(EPS[:, 0:fine], 1e-6).then_inc(S["const_set"], 1)
            pool.memset(EPS[:, fine:], 1e-5).then_inc(S["const_set"], 1)
            pool.memset(LSC[:, :, :], 1.0).then_inc(S["lset"], 1)
            pool.memset(LSH[:, :, :], 0.0).then_inc(S["lset"], 1)
            pool.memset(ONE[:, :], 0.0).then_inc(S["const_set"], 1)
            pool.memset(CM[:, :, :], 0.0).then_inc(S["const_set"], 1)
            pool.wait_ge(S["const_set"], 5)
            pool.memset(ONE[0:1, :], 1.0).then_inc(S["const_set"], 1)
            pool.memset(QH[:, :, :, :], 0.0).then_inc(S["const_set"], 1)
            pool.memset(VXC[:, :, :, :], 0.0).then_inc(S["const_set"], 1)
            pool.memset(MHL[:, :, :], 0.0).then_inc(S["const_set"], 1)
            pool.wait_ge(w_in[0], 16)
            for at in (WQ, CQ):
                pool.tensor_scalar(wl(0, at), wl(0, at), SCALE, None, ALU.mult).then_inc(S["wq_scaled"], 1)
            for k in range(4):
                pool.wait_ge(x_in[k], 16)
            hold().then_inc(S["x_ready"], GROUPS)

            def moments(u):
                n = u.n()
                wait(pool, "ln_moments", n + 1)
                pool.tensor_tensor(VE[:, :], MV[:, :, 1], EPS[:, bass.ds(n * GB, GB)], ALU.add).then_inc(S["var_eps"], 1)
                wait(pool, "var_eps", n + 1)
                pool.tensor_tensor(RSTD[:, :], VE[:, :], NHALF[:, 0:GB], ALU.pow).then_inc(S["rstd_ready"], 1)

            def context(u):
                wait(pool, "v_psum", u.n("att"))
                hold()
                src = CTXN if u.layer == 0 else CTXT
                pool.tensor_copy(CG[:, u.par, :], src[:, bass.ds(C * u.seq(), GB * C)]).then_inc(S["cg_ready"], 1)

            def third_part(u):
                a, end = u.n("att"), width(u)
                wait(pool, "part2", a + 1)
                pool.tensor_tensor(PT[:, 2, 0:end], R1[:, 0:end], PT[:, 1, 0:end], ALU.subtract)\
                    .then_inc(S["part3"], 1)

            def masks(u):
                wait(pool, "p_ready", 4 * (u.n("att") - 1))
                hold()
                pool.tensor_copy(CMG[:, u.par, :, :], CM[:, bass.ds(u.seq(), GB), :]).then_inc(S["cm_ready"], 1)
                pool.tensor_copy(CMTG[:, u.par, :], CMT[:, bass.ds(u.seq(), GB)]).then_inc(S["cm_ready"], 1)

            def add(u):
                mine = bass.ds(u.seq(), GB)
                wait(pool, "yt_ready", u.n() + 1)
                if u.p["gate"] is not None:
                    wait(pool, "gate_in", 16 * (u.n("gated") + 1))
                    pool.tensor_tensor(YT[:, u.par, :, :], YT[:, u.par, :, :], GATE[:, u.par, :, :], ALU.mult)\
                        .then_inc(S["gated"], 1)
                    wait(pool, "gated", u.n("gated") + 1)
                pool.tensor_tensor(X[:, mine, :], X[:, mine, :], YT[:, u.par, :, :], ALU.add).then_inc(S["x_ready"], 1)

            def unit(prev, u, nxt, nxt2, rows):
                if nxt and nxt.kind == CROSS and nxt.p["mask"]:
                    masks(nxt)
                if rows:
                    moments(rows)
                if nxt2 and nxt2.attends:
                    third_part(nxt2)
                if nxt2 and nxt2.kind == CROSS:
                    context(nxt2)
                if prev:
                    add(prev)

            alone(unit, -3)
            pool.wait_ge(S["cmoments"], 1)
            pool.tensor_tensor(CVE[:, 0, :], CMV[:, :, 1], EPS[0:C, 0:B], ALU.add).then_inc(S["cvar"], 1)
            pool.wait_ge(S["cvar"], 1)
            pool.tensor_tensor(CVE[:, 1, :], CVE[:, 0, :], NHALF[0:C, :], ALU.pow).then_inc(S["crstd"], 1)
            alone(unit, -2)
            alone(unit, -1)
            for layer in range(1, NLAYER):
                pool.wait_ge(w_in[layer], 16)
                for at in (WQ, CQ):
                    pool.tensor_scalar(wl(layer, at), wl(layer, at), SCALE, None, ALU.mult)\
                        .then_inc(S["wq_scaled"], 1)
            pool.wait_ge(S["wrot_in"], 16)
            for k in range(NROPE):
                pool.tensor_scalar(WR[:, k, 0, :], WR[:, k, 0, :], SCALE, None, ALU.mult)\
                    .then_inc(S["wq_scaled"], 1)
            pool.wait_ge(S["ct_ready"], len(CBANKS))
            pool.wait_ge(S["ctxt_in"], 16)
            pool.wait_ge(S["mask_ready"], 3)
            run(pool, unit)

        @block.vector
        def _(dve):
            dve.memset(KH[:, :, :], 0.0).then_inc(S["kh_zero"], 1)
            dve.wait_ge(S["silu_exp"], 1)
            dve.tensor_scalar(CT[:, 1, :], CT[:, 0, :], 1.0, None, ALU.add).then_inc(S["silu_step"], 1)
            dve.wait_ge(S["silu_step"], 1)
            dve.reciprocal(CT[:, 2, :], CT[:, 1, :]).then_inc(S["silu_step"], 1)
            dve.wait_ge(S["silu_step"], 2)
            dve.tensor_tensor(CS[:, 0, :], CS[:, 1, :], CT[:, 2, :], ALU.mult).then_inc(S["cond_ready"], 1)
            dve.wait_ge(S["modb_in"], 32)
            for part, dst in ((0, SCL), (1, SHF)):
                if part:
                    dve.wait_ge(S["ctx_in"], 16)
                    for b in range(B):
                        last = dve.bn_stats(CST[:, b, :], CRAW[0:C, b, :])
                    last.then_inc(S["cstats"], 1)
                    dve.wait_ge(S["cstats"], 1)
                    for b in range(B):
                        last = dve.bn_aggr(CMV[:, b, :], CST[:, b, :])
                    last.then_inc(S["cmoments"], 1)
                dve.wait_ge(S["mod_psum"], part + 1)
                dve.tensor_tensor(dst[:, :, :],
                                  PY[:, part * 256:part * 256 + NMOD * B].rearrange("p (s b) -> p s b", b=B),
                                  MODB[:, part * NMOD:(part + 1) * NMOD].unsqueeze(2).to_broadcast([D, NMOD, B]),
                                  ALU.add).then_inc(S["mod_step"], 1)
            dve.wait_ge(S["mod_step"], 1)
            dve.tensor_scalar(SCL[:, :, :], SCL[:, :, :], 1.0, None, ALU.add).then_inc(S["mod_step"], 1)
            dve.wait_ge(S["mod_step"], 3)
            dve.tensor_tensor(SCL[:, NMOD - 3:NMOD, :], SCL[:, NMOD - 3:NMOD, :],
                              NORMW[:, :].unsqueeze(2).to_broadcast([D, 3, B]), ALU.mult).then_inc(S["mods_ready"], 1)
            dve.wait_ge(S["mods_ready"], 1)
            dve.wait_ge(S["lset"], 2)
            runs = []
            for n, p in enumerate(PHASES):
                if p["mod"] is not None:
                    if n and PHASES[n - 1]["mod"] is not None:
                        runs[-1][2] += 1
                    else:
                        runs.append([n, p["mod"], 1])
            for dst, src in ((LSC, SCL), (LSH, SHF)):
                for to, at, many in runs:
                    dve.tensor_copy(dst[:, to:to + many, :], src[:, at:at + many, :]).then_inc(S["ls_ready"], 1)
            def stats(u):
                n = u.n()
                wait(dve, "x_ready", n + 1)
                for b in range(GB):
                    ins = dve.bn_stats(ST[:, b, :], X[:, bass.ds(u.seq(b), 1), :])
                ins.then_inc(S["ln_stats"], 1)
                wait(dve, "ln_stats", n + 1)
                dve.tensor_copy(HOLD[:, :], ST[:, 0, 0:1])
                for b in range(GB):
                    ins = dve.bn_aggr(MV[:, b, :], ST[:, b, :])
                ins.then_inc(S["ln_moments"], 1)

            def normalise(u):
                n = u.n()
                wait(dve, "rstd_ready", n + 1)
                wait(dve, "xnt_psum", n)
                for b in range(GB):
                    ins = dve.tensor_scalar(XN[:, b, :], X[:, bass.ds(u.seq(b), 1), :], MV[:, b, 0:1],
                                            RSTD[:, b:b + 1], ALU.subtract, ALU.mult)
                ins.then_inc(S["xn_ready"], 1)

            def residual(u):
                n = u.n()
                wait(dve, "y_psum", n + 1)
                wait(dve, "x_ready", n - 1 + GROUPS)
                y = PY[:, 0:GB * D].rearrange("p (b d) -> p b d", b=GB)
                if u.p["bias"] is None:
                    dve.tensor_copy(YT[:, u.par, :, :], y).then_inc(S["yt_ready"], 1)
                else:
                    row = ROWB[:, u.p["bias"]:u.p["bias"] + 1, :].to_broadcast([N, GB, D])
                    dve.tensor_tensor(YT[:, u.par, :, :], y, row, ALU.add).then_inc(S["yt_ready"], 1)

            def v_tiles(u):
                a = u.n("att")
                wait(dve, "v_psum", a + 1)
                dst = VX if u.kind == SELF else VXC
                k = u.p["att0"] // GROUPS
                dve.tensor_tensor(dst[0:u.T, u.par, :, :], POA[0:u.T, 0:GB * VC].rearrange("p (b c) -> p b c", b=GB),
                                  ROWV[0:u.T, k:k + 1, :].to_broadcast([u.T, GB, VC]), ALU.add)\
                   .then_inc(S["v_ready"], 1)

            def rotate(u):
                a, end, r = u.n("att"), width(u), u.p["rope"]
                wait(dve, "qk_psum", a + 1)
                dve.tensor_tensor(T1[:, 0:end], POB[:, 0:end], RC[:, r, 0:end], ALU.mult)\
                   .then_inc(S["rope_parts"], 1)
                dve.tensor_tensor(T2[:, 0:end], TR[:, 0:end], RS[:, r, 0:end], ALU.mult)\
                   .then_inc(S["rope_parts"], 1)
                wait(dve, "rope_parts", 2 * (u.n("rope") + 1))
                dve.tensor_tensor(QKT[:, 0:end], T1[:, 0:end], T2[:, 0:end], ALU.add).then_inc(S["rotated"], 1)

            def rest(u):
                a, end = u.n("att"), width(u)
                wait(dve, "part1", a + 1)
                wait(dve, "part3", a)
                if u.p["qk"] is None:
                    src = POB if u.p["rope"] is None else QKT
                    dve.tensor_tensor(R1[:, 0:end], src[:, 0:end], PT[:, 0, 0:end], ALU.subtract)\
                       .then_inc(S["rest1"], 1)
                    return
                for k, (lo, hi) in enumerate(((0, TOK), (TOK, end))):
                    c = u.p["qk"] + k
                    last = dve.scalar_tensor_tensor(out=R1[:, lo:hi], in0=POB[:, lo:hi], scalar=COLB[:, c:c + 1],
                                                    in1=PT[:, 0, lo:hi], op0=ALU.add, op1=ALU.subtract)
                last.then_inc(S["rest1"], 1)

            def maxima(u, k, wide):
                wait(dve, "s_psum", 4 * u.n("att") + k + 1)
                first = 2 * (wide and k % 2)
                bank = SC[:, first:first + 2, 0:HG * u.T].rearrange("p g (h k) -> p g h k", h=HG)
                dve.tensor_reduce(MX[:, 8 * k:8 * k + 8].rearrange("p (g h) -> p g h", g=2), bank, AX.X, ALU.max)\
                   .then_inc(S["mx_ready"], 1)

            def divide(u, b):
                k = 2 * u.n("att") + b
                wait(dve, "tr_psum", k + 1)
                dve.reciprocal(RDEN[:, :], sums).then_inc(S["rden_ready"], 1)
                wait(dve, "rden_ready", k + 1)
                dve.tensor_tensor(OQ[:, b, 0:96].rearrange("p (i t d) -> p i t d", i=3, t=4), own_a,
                                  RDEN[:, 0:12].rearrange("p (i t) -> p i t", i=3).unsqueeze(3)
                                  .to_broadcast([N, 3, 4, HD]), ALU.mult)
                dve.tensor_tensor(OQ[:, b, 96:128].rearrange("p (i t d) -> p i t d", i=2, t=2), own_b,
                                  RDEN[:, 12:16].rearrange("p (i t) -> p i t", i=2).unsqueeze(3)
                                  .to_broadcast([N, 2, 2, HD]), ALU.mult).then_inc(S["oq_ready"], 1)

            def outputs(u, b):
                wait(dve, "o_psum", 2 * u.n("att") + b + 1)
                dve.tensor_copy(OSB[:, b, :], POB[0:N // 2, 0:2 * N]).then_inc(S["ob_ready"], 1)

            def negated(u):
                a = u.n("att")
                wait(dve, "mx_ready", 4 * (a + 1))
                dve.tensor_scalar(MHL[:, 0, 0:GB * H], MX[:, :], -1.0, None, ALU.mult).then_inc(S["neg_hi"], 1)
                wait(dve, "neg_hi", a + 1)
                dve.scalar_tensor_tensor(out=MHL[:, 1, 0:GB * H], in0=MX[:, :], scalar=-1.0, in1=MHL[:, 0, 0:GB * H],
                                         op0=ALU.mult, op1=ALU.subtract).then_inc(S["neg_ready"], 1)

            def spread(u):
                a = u.n("att")
                wait(dve, "m_psum", a + 1)
                dve.tensor_tensor(MBD[:, u.par, :, :], PYM.unsqueeze(1).to_broadcast([N, HG, N]),
                                  J4[:, :].unsqueeze(2).to_broadcast([N, HG, N]), ALU.mult).then_inc(S["mbd_ready"], 1)

            def unit(prev, u, nxt, nxt2, rows):
                late = prev and prev.attends
                now = u and u.attends
                soon = nxt and nxt.attends
                ahead = nxt2 and nxt2.attends
                if rows:
                    stats(rows)
                if soon:
                    v_tiles(nxt)
                turned = ahead and nxt2.p["rope"] is not None
                if turned:
                    rotate(nxt2)
                if late and not turned:
                    divide(prev, 0)
                inside = not now and not late
                if prev and inside:
                    residual(prev)
                if ahead and not now:
                    rest(nxt2)
                if soon:
                    maxima(nxt, 0, not now)
                if ahead and now:
                    rest(nxt2)
                if late:
                    divide(prev, 0 if turned else 1)
                if rows:
                    normalise(rows)
                if soon:
                    maxima(nxt, 1, not now)
                if late and turned:
                    divide(prev, 1)
                if now:
                    outputs(u, 0)
                if soon:
                    maxima(nxt, 2, not now)
                if prev and not inside:
                    residual(prev)
                if soon:
                    maxima(nxt, 3, not now)
                    negated(nxt)
                if now:
                    outputs(u, 1)
                if soon:
                    spread(nxt)

            alone(unit, -3)
            dve.wait_ge(S["gatew_in"], 32)
            for k, (lo, hi) in enumerate(((0, 4 * D), (4 * D, NGATE * D))):
                dve.wait_ge(S["g_psum"], k + 1)
                dve.tensor_tensor(G[:, 1, lo:hi], (POA, POB)[k][0:B, 0:hi - lo], G[:, 0, lo:hi], ALU.add)\
                   .then_inc(S["g_ready"], 1)
            dve.wait_ge(S["small_in"], 16 * NSMALL)
            dve.wait_ge(S["const_set"], 5)
            for dst, src in ((SM[:, :], MU8[:, 0:N]), (CMT[:, :], MU8[0:C, N:N + B]),
                             (CM[0:1, :, :], CM8[:, :].rearrange("p (b c) -> p b c", b=B))):
                dve.tensor_scalar(dst, src, -1.0, BIG, ALU.add, ALU.mult).then_inc(S["mask_ready"], 1)
            for k in (0, 2, 4, 6):
                dve.tensor_scalar(COLB[:, k:k + 1], COLB[:, k:k + 1], SCALE, None, ALU.mult).then_inc(S["mask_ready"], 1)

            dve.wait_ge(S["const_in"], 16 * NCONST)
            dve.wait_ge(S["rows_in"], 32)
            dve.wait_ge(S["const_set"], 9)
            dve.wait_ge(S["gate_out"], 16)
            alone(unit, -2)
            dve.wait_ge(S["cmoments"], 1)
            dve.wait_ge(S["crstd"], 1)
            for b in range(B):
                last = dve.tensor_scalar(CRAW[0:C, b, :], CRAW[0:C, b, :], CMV[:, b, 0:1], CVE[:, 1, b:b + 1],
                                         ALU.subtract, ALU.mult)
            last.then_inc(S["cn_ready"], 1)
            alone(unit, -1)
            run(dve, unit)

        @block.tensor
        def _(pe):
            def mm(o, l, r, start=True, stop=True, **more):
                return pe.matmul(o, l, r, start=start, stop=stop, **more)

            pe.wait_ge(S["cond_ready"], 1)
            for part in range(2):
                pe.wait_ge(S["mods_in"], 32)
                if part:
                    pe.wait_ge(S["mod_step"], 1)
                for k in range(NMOD):
                    at = part * 256 + k * B
                    last = mm(PY[:, at:at + B], MODW[:, part, k * D:k * D + D], CS[:, 0 if k < 4 else 1, :])
                last.then_inc(S["mod_psum"], 1)
            pe.wait_ge(S["gatew_in"], 32)
            mm(POA[0:B, 0:4 * D], CS[:, 0, :], GATEW[:, 0:4 * D]).then_inc(S["g_psum"], 1)
            mm(POB[0:B, 0:3 * D], CS[:, 1, :], GATEW[:, 4 * D:7 * D]).then_inc(S["g_psum"], 1)
            pe.wait_ge(S["const_in"], 16 * NCONST)

            def normed(u):
                wait(pe, "xnt_ready", GB * u.n())
                wait(pe, "xn_ready", u.n() + 1)
                for b in range(GB):
                    last = pe.transpose(TR[:, b * N:b * N + N], XN[:, b, :], ID[:, :])
                last.then_inc(S["xnt_psum"], 1)

            def source(u):
                return XNT[:, u.par, :] if u.kind == SELF else CG[:, u.par, :]

            def project_v(u):
                wait(pe, "oa_ready", 2 * (u.n("att") - 1))
                if u.kind == CROSS:
                    wait(pe, "cg_ready", u.n("cross") + 1)
                for b in range(GB):
                    last = mm(POA[0:u.T, b * VC:b * VC + VC], source(u)[:, b * u.T:b * u.T + u.T],
                              wl(u.layer, weights(u)[2], VC))
                last.then_inc(S["v_psum"], 1)

            def project_qk(u):
                wq, wk = [wl(u.layer, k) for k in weights(u)[:2]]
                x, end = XNT[:, u.par, :], width(u)
                src = x
                if u.kind == CROSS:
                    src = (CTXN if u.layer == 0 else CTXT)[:, bass.ds(C * u.seq(), GB * C)]
                wait(pe, "xnt_ready", GB * (u.n() + 1))
                wait(pe, "ob_ready", 2 * (u.n("att") - 2))
                if isinstance(u.i, int) and u.i == 0:
                    layer = u.layer
                    pe.wait_ge(w_in[layer], 16)
                    pe.wait_ge(S["wq_scaled"], 2 * layer + 2 if layer < 2 else 2 * NLAYER + NROPE)
                    if u.kind == CROSS:
                        pe.wait_ge(S["ctxt_in"], 16)
                last = mm(POB[:, 0:TOK], wq, x)
                last = mm(POB[:, TOK:end], wk, src)
                if u.p["rope"] is not None:
                    mm(TR[:, 0:TOK], WR[:, u.p["rope"], 0, :], x)
                    last = mm(TR[:, TOK:end], WR[:, u.p["rope"], 1, :], src)
                last.then_inc(S["qk_psum"], 1)

            def keys(u, h, b):
                k = KH[:, u.par, 0:H * GB * u.T].rearrange("p (h t) -> p h t", h=H)
                return k[:, h, b * u.T:b * u.T + u.T]

            def scores(u, k, wide):
                b, a = k // 2, u.n("att")
                if k == 0:
                    wait(pe, "qk_in", LOADS * (a + 1))
                    if u.p["mask"] and u.kind == CROSS:
                        wait(pe, "cm_ready", 2 * (u.i + 1))
                wait(pe, "mx_ready", 4 * a + k - (wide and k > 0))
                masked = u.p["mask"]
                for bank in range(2):
                    g = 2 * (k % 2) + bank
                    whole = SC[:, 2 * (wide and k % 2) + bank, 0:HG * u.T].rearrange("p (h k) -> p h k", h=HG)
                    if masked and u.kind == SELF:
                        mm(whole, IDB[:, :], SM[:, :].unsqueeze(1).to_broadcast([N, HG, N]), stop=False,
                           skip_group_check=True)
                    elif masked:
                        mm(whole, ONE[:, :], CMG[:, u.par, b:b + 1, :].to_broadcast([N, HG, C]), stop=False,
                           skip_group_check=True)
                    for j in range(HG):
                        last = mm(whole[:, j, :], QH[:, u.par, HG * g + j, b * N:b * N + N], keys(u, HG * g + j, b),
                                  start=not masked, skip_group_check=masked)
                last.then_inc(S["s_psum"], 1)

            def shifted(u, k):
                b, pr = divmod(k, 2)
                a = u.n("att")
                wait(pe, "p_ready", 4 * a + k)
                masked = u.p["mask"] and u.kind == SELF
                for bank in range(2):
                    g = 2 * pr + bank
                    dst = SC[0:u.T, 2 + bank, :].rearrange("p (h q) -> p h q", h=HG)
                    if masked:
                        mm(dst, SM[:, :], IDB[:, :].unsqueeze(1).to_broadcast([N, HG, N]), stop=False,
                           skip_group_check=True)
                    else:
                        mm(dst, SEL[:, NHG * b + g, 0:u.T], MBD[:, u.par, :, :], stop=False, skip_group_check=True)
                    for j in range(HG):
                        last = mm(dst[:, j, :], keys(u, HG * g + j, b), QH[:, u.par, HG * g + j, b * N:b * N + N],
                                  start=False, stop=not masked, skip_group_check=True)
                    if masked:
                        last = mm(dst, SEL[:, NHG * b + g, 0:u.T], MBD[:, u.par, :, :], start=False, skip_group_check=True)
                last.then_inc(S["st_psum"], 1)

            def values(u, b):
                wait(pe, "p_ready", 4 * u.n("att") + 2 * b + 2)
                v = (VX if u.kind == SELF else VXC)[:, u.par, b, :]
                for t, heads in enumerate(TILE_HEADS):
                    bank, row = (POA, t) if t < 4 else (POB, t - 4)
                    n = len(heads) * N
                    last = mm(bank[VW * row:VW * row + VW, 0:n], v[:, VW * t:VW * t + VW],
                              PR[:, b, heads[0] * N:heads[0] * N + n])
                last.then_inc(S["o_psum"], 1)

            def to_rows(u, b):
                k = 2 * u.n("att") + b
                wait(pe, "oa_ready", k + 1)
                wait(pe, "ob_ready", k + 1)
                for i in range(3):
                    pe.transpose(TR[:, i * N:i * N + N], OSA[:, b, i * N:i * N + N], ID[:, :])
                for i in range(2):
                    at = 3 * N + i * N // 2
                    last = pe.transpose(TR[:, at:at + N // 2], OSB[:, b, i * N:i * N + N], ID[0:N // 2, 0:N // 2])
                last.then_inc(S["tr_psum"], 1)

            def to_features(u, b):
                wait(pe, "oq_ready", 2 * u.n("att") + b + 1)
                pe.transpose(PYOT, OQ[:, b, :], ID[:, :]).then_inc(S["ot_psum"], 1)

            def project_out(u, b):
                wait(pe, "ot_ready", 2 * u.n("att") + b + 1)
                last = mm(PY[:, b * D:b * D + D], OT[:, b, :], wl(u.layer, weights(u)[3]))
                if b == GB - 1:
                    last.then_inc(S["y_psum"], 1)

            def hidden(u, chunks):
                for c in chunks:
                    wait(pe, "h_ready", NC * (u.n("mlp") - 1) + c + 1)
                    mm(SC[:, c, 0:TOK], wl(u.layer, W1 + c * D), XNT[:, u.par, :]).then_inc(S["h_psum"], 1)

            def mlp_out(u):
                wait(pe, "h_ready", NC * (u.n("mlp") + 1))
                wait(pe, "yt_ready", u.n())
                for b in range(GB):
                    for c in range(NC):
                        last = mm(PY[:, b * D:b * D + D], HT[:, u.par, c, b * N:b * N + N], wl(u.layer, W2 + c * D),
                                  start=c == 0, stop=c == NC - 1)
                last.then_inc(S["y_psum"], 1)

            def unit(prev, u, nxt, nxt2, rows):
                late = prev and prev.attends
                now = u and u.attends
                soon = nxt and nxt.attends
                ahead = nxt2 and nxt2.attends
                turned = ahead and nxt2.p["rope"] is not None
                if ahead:
                    project_qk(nxt2)
                if now:
                    wait(pe, "mbd_ready", u.n("att") + 1)
                    shifted(u, 0)
                if nxt and not soon and not now:
                    wait(pe, "xnt_ready", GB * (nxt.n() + 1))
                    hidden(nxt, range(NC))
                if late:
                    if nxt2:
                        wait(pe, "xnt_ready", GB * (nxt2.n() + 1))
                    if not turned:
                        to_rows(prev, 0)
                if u and not now and soon:
                    mlp_out(u)
                if soon:
                    scores(nxt, 0, not now)
                if late and not turned:
                    wait(pe, "yt_ready", prev.n())
                    to_features(prev, 0)
                if now:
                    shifted(u, 1)
                if late and turned:
                    wait(pe, "rope_parts", 2 * (nxt2.n("rope") + 1))
                    to_rows(prev, 0)
                if late and not turned:
                    project_out(prev, 0)
                    to_rows(prev, 1)
                if soon:
                    scores(nxt, 1, not now)
                if late and turned:
                    wait(pe, "yt_ready", prev.n())
                    to_features(prev, 0)
                if now:
                    shifted(u, 2)
                if late and turned:
                    project_out(prev, 0)
                    to_rows(prev, 1)
                if now:
                    if soon:
                        wait(pe, "v_ready", nxt.n("att") + 1)
                    if ahead:
                        wait(pe, "rest1", nxt2.n("att") + 1)
                    values(u, 0)
                if late:
                    to_features(prev, 1)
                if soon:
                    scores(nxt, 2, not now)
                if now:
                    shifted(u, 3)
                if late:
                    project_out(prev, 1)
                if u and not now and not soon:
                    mlp_out(u)
                lone = nxt and not soon and now
                if rows and not lone:
                    if ahead and not late:
                        wait(pe, "rest1", nxt2.n("att") + 1)
                    normed(rows)
                if soon:
                    scores(nxt, 3, not now)
                if now:
                    wait(pe, "oa_ready", 2 * u.n("att") + 1)
                    wait(pe, "ob_ready", 2 * u.n("att") + 1)
                    values(u, 1)
                if soon:
                    wait(pe, "neg_ready", nxt.n("att") + 1)
                    pe.transpose(PYM, MHL[:, :, :].rearrange("p a c -> p (a c)"), IDB[:, :]).then_inc(S["m_psum"], 1)
                if ahead:
                    project_v(nxt2)
                if lone:
                    wait(pe, "xnt_ready", GB * (nxt.n() + 1))
                    hidden(nxt, range(NC))
                    if rows:
                        normed(rows)

            alone(unit, -3)
            pe.wait_ge(S["mod_step"], 3)
            pe.wait_ge(S["g_ready"], 2)
            pe.wait_ge(S["const_set"], 9)
            alone(unit, -2)
            pe.wait_ge(S["cn_ready"], 1)
            for k, (lo, hi) in enumerate(CBANKS):
                for b in range(lo, hi):
                    last = pe.transpose(SC[:, k, C * (b - lo):C * (b - lo + 1)], CRAW[0:C, b, :], ID[0:C, 0:C])
                last.then_inc(S["ct_psum"], 1)
            pe.wait_ge(S["ct_ready"], len(CBANKS))
            alone(unit, -1)
            run(pe, unit)


def kernel(**inputs):
    import ml_dtypes
    import concourse.bacc as bacc
    from concourse.bass_utils import run_bass_kernel_spmd

    t = {k: np.asarray(v) for k, v in inputs.items()}
    L = [{k[9:]: v for k, v in t.items() if k.startswith(f"L{n}_xcond_")} for n in range(4)]
    a, b, c, d = L

    def cut(m, n):
        return m[..., n * D:(n + 1) * D]

    by_width = np.arange(D).reshape(H, HD).T.reshape(-1)
    swap = np.arange(D).reshape(H, 2, HD // 2)[:, ::-1].reshape(-1)[by_width]
    outs = np.concatenate([np.arange(h * HD, h * HD + HD) for h in OUT_HEADS])

    def tiles(m, one=0.0):
        r = np.zeros(m.shape[:-1] + (VT, VW), m.dtype)
        for k, heads in enumerate(TILE_HEADS):
            r[..., k, 0:HD * len(heads)] = m[..., heads[0] * HD:(heads[-1] + 1) * HD]
        r[..., ONE_AT] = one
        return r.reshape(m.shape[:-1] + (VC,))

    def blocks(wt):
        return np.concatenate([wt[k * D:k * D + D] for k in range(NC)], axis=1)

    def layer(q, k, v, o, cq, ck, cv, co, w1, w2):
        return np.concatenate([q[:, by_width], k[:, by_width], tiles(v), o[outs], cq[:, by_width], ck[:, by_width],
                               tiles(cv), co[outs], w1, blocks(w2)], axis=1)

    qkv2 = c["qkv_w"].T
    w = np.stack([
        layer(*[cut(a["W_qkv"], n) for n in range(3)], a["W_proj"], a["W_qc"], cut(a["W_kvc"], 0), cut(a["W_kvc"], 1),
              a["W_cproj"], a["W_mlp1"], a["W_mlp2"]),
        layer(*[cut(b["qkv_w"], n) for n in range(3)], b["sa_proj_w"], b["q_w"], cut(b["kv_w"], 0), cut(b["kv_w"], 1),
              b["ca_proj_w"], b["fc1_w"], b["fc2_w"]),
        layer(*[cut(qkv2, n) for n in range(3)], c["sa_out_w"].T, c["q_w"].T, c["k_w"].T, c["v_w"].T,
              c["ca_out_w"].T, c["ffn_w1"].T, c["ffn_w2"].T),
        layer(*[cut(d["qkv_W"], n) for n in range(3)], d["attn_out_W"], d["cq_W"], d["ck_W"], d["cv_W"],
              d["co_W"], d["mlp_W1"], d["mlp_W2"]),
    ])
    wrot = np.stack([m[:, swap] for m in (cut(qkv2, 0), cut(qkv2, 1), c["q_w"].T, c["k_w"].T, cut(d["qkv_W"], 0),
                                          cut(d["qkv_W"], 1))], axis=1).reshape(D, NROPE, 2, D)

    lns = [(c[f"ln{k}_w"].T, c[f"ln{k}_b"]) for k in (1, 2, 3)]
    scale = [(a["W_mod"], a["b_mod"], 1), (a["W_mod"], a["b_mod"], 4), (b["adaln_w"], b["adaln_b"], 1),
             (b["adaln_w"], b["adaln_b"], 4)] + [(x, y, 0) for x, y in lns] + \
            [(d["adaLN_W"], d["adaLN_b"], k) for k in (1, 4, 7)]
    shift = [(a["W_mod"], a["b_mod"], 0), (a["W_mod"], a["b_mod"], 3), (b["adaln_w"], b["adaln_b"], 0),
             (b["adaln_w"], b["adaln_b"], 3)] + [(x, y, 1) for x, y in lns] + \
            [(d["adaLN_W"], d["adaLN_b"], k) for k in (0, 3, 6)]
    gate = [(a["W_mod"], a["b_mod"], 2), (a["W_mod"], a["b_mod"], 5), (b["adaln_w"], b["adaln_b"], 2),
            (b["adaln_w"], b["adaln_b"], 5)] + [(d["adaLN_W"], d["adaLN_b"], k) for k in (2, 5, 8)]
    modw = np.concatenate([cut(x, n) for x, _, n in scale + shift], axis=1)
    modb = np.stack([cut(y, n) for _, y, n in scale + shift], axis=1)
    gatew = np.concatenate([cut(x, n) for x, _, n in gate], axis=1)
    gateb = np.concatenate([cut(y, n) for _, y, n in gate])
    colb = np.stack([m[by_width] for m in (cut(a["b_qkv"], 0), cut(a["b_qkv"], 1), a["b_qc"], cut(a["b_kvc"], 0),
                                           cut(b["qkv_b"], 0), cut(b["qkv_b"], 1), b["q_b"], cut(b["kv_b"], 0))],
                    axis=1)
    rowb = np.stack([a["b_proj"], a["b_cproj"], a["b_mlp2"], b["sa_proj_b"], b["ca_proj_b"], b["fc2_b"],
                     c["ffn_b2"], d["mlp_b2"]])
    rowv = np.stack([tiles(m, 1.0) for m in (cut(a["b_qkv"], 2), cut(a["b_kvc"], 1), cut(b["qkv_b"], 2),
                                             cut(b["kv_b"], 1))] + [tiles(np.zeros(D, np.float32), 1.0)] * 4)
    mlpb = np.stack([x.reshape(NC, D).T for x in (a["b_mlp1"], b["fc1_b"], c["ffn_b1"], d["mlp_b1"])], axis=1)

    row = np.arange(N)
    jmask4 = (row[:, None] % HG == np.arange(HG)).astype(np.float32)
    sel = np.repeat((row[:, None] % (N // 2) // HG == np.arange(GB * NHG))[:, :, None], N, axis=2)\
        .astype(ml_dtypes.bfloat16)
    half = HD // 2
    width = row // H
    freq = (1.0 / 10000.0 ** (np.arange(half, dtype=np.float32) / half)).astype(np.float32)[width % half]
    tok = np.arange(N)
    pos = np.zeros((NROPE, 2 * TOK), np.float32)
    pos[0] = np.tile(tok, 2 * GB)
    pos[1, :TOK] = np.tile(tok, GB)
    pos[1, TOK:TOK + GB * C] = np.tile(np.arange(C), GB)
    pos[2] = np.tile(tok % (N // 2), 2 * GB)
    ang = freq[:, None, None] * pos[None]
    sign = np.where(width < half, -1.0, 1.0).astype(np.float32)[:, None, None]
    arrays = dict(
        x=t["x"], cond_t=t["cond_1024"].T, ctx_tok=t["ctx_1024"], ctx_t=t["ctx_1024"].reshape(B * C, D).T,
        w=w, wrot=wrot, modw=modw, modb=modb, gatew=gatew, gateb=gateb,
        normw=np.stack([d["norm1_w"], d["normc_w"], d["norm2_w"]], axis=1), colb=colb, rowb=rowb, rowv=rowv,
        mlpb=mlpb, smask=t["mask_SxS_bk0"], cmask=t["mask_BxS2_bf1"].reshape(1, B * C),
        cmask_t=t["mask_BxS2_bf1"].T,
        ident=np.eye(N, dtype=np.float32), identb=np.eye(N, dtype=np.float32).astype(ml_dtypes.bfloat16),
        jmask4=jmask4, sel=sel,
        ropec=np.cos(ang).astype(np.float32), ropes=(np.sin(ang) * sign).astype(np.float32))
    arrays = {"in_" + k: np.ascontiguousarray(v) for k, v in arrays.items()}
    nc = bacc.Bacc("TRN2", target_bir_lowering=False, num_devices=1)
    args = {k[3:]: nc.dram_tensor(k, v.shape, mybir.dt.from_np(v.dtype), kind="ExternalInput").ap()
            for k, v in arrays.items()}
    out = nc.dram_tensor("out", (B, N, D), F32, kind="ExternalOutput").ap()
    build(nc, out=out, **args)
    r = run_bass_kernel_spmd(nc, [arrays], core_ids=[0])
    return r.results[0]["out"]
```
